# Optimizing a Trainium2 kernel written in Bass

```python
import numpy as np
import jax
import jax.numpy as jnp

def _softmax(x, axis=-1):
    return jax.nn.softmax(x, axis=axis)

def _gelu(x):
    return jax.nn.gelu(x, approximate=True)

def _silu(x):
    return jax.nn.silu(x)

def _sigmoid(x):
    return jax.nn.sigmoid(x)

def _layernorm(x, axis=-1, eps=1e-05):
    m = jnp.mean(x, axis=axis, keepdims=True)
    v = jnp.var(x, axis=axis, keepdims=True)
    return (x - m) / jnp.sqrt(v + eps)

def _scatter_add(tgt, idx, src, axis=0):
    return tgt.at[idx].add(src)

def _segment_sum(src, seg, n):
    return jax.ops.segment_sum(src, seg, n)
kernel_name = 'mk_adj_ffn_d1_adj_r2_af446a'

def setup_inputs(seed: int=0):
    np.random.seed(seed)
    _w = jnp.asarray

    def _rec_inputs():
        import jax
        import jax.numpy as jnp
        _gk = jax.random.key(seed)
        x = -0.0005146 + 1 * jax.random.normal(jax.random.fold_in(_gk, 1), (8, 1024, 128), jnp.float32)
        _a = jax.random.bernoulli(jax.random.fold_in(_gk, 2), 0.015625, (8, 1024, 1024))
        adj = _a.astype(jnp.int32)
        return (x, adj)
    x, adj = _rec_inputs()

    def _L0_gnn_setup():
        import jax, jax.numpy as jnp
        import numpy as np
        B, N, C, OUT, S = (4, 1024, 128, 128, 25)
        DENSITY = 0.008
        key = jax.random.key(seed)
        kA, kX, kW = jax.random.split(key, 3)
        A = jax.random.bernoulli(kA, DENSITY, (B, N, N)).astype(jnp.int32)
        X = jax.random.normal(kX, (B, N, C), dtype=jnp.float32)
        W = jax.random.normal(kW, (2 * C, OUT), dtype=jnp.float32) * np.float32(1.0 / np.sqrt(2 * C))
        b = jnp.zeros((OUT,), dtype=jnp.float32)
        return {'A': A, 'X': X, 'W': W, 'b': b}
    _L0_gnn_all = _L0_gnn_setup()
    _L0_gnn_in = {k: v for k, v in _L0_gnn_all.items() if k in ('W', 'b')}
    del _L0_gnn_all

    def _L0_ffn_setup():
        import jax, jax.numpy as jnp
        import numpy as np
        B, S, H, NH, NE = (4, 512, 128, 4, 4)
        D = H // NH
        EPS = 1e-08

        def layernorm(x, g, b):
            m = jnp.mean(x, axis=-1, keepdims=True)
            v = jnp.mean((x - m) ** 2, axis=-1, keepdims=True)
            return (x - m) / jnp.sqrt(v + EPS) * g + b
        key = jax.random.key(seed)
        ks = jax.random.split(key, 18)
        sc = 0.05
        return {'x': jax.random.normal(ks[0], (B, S, H), jnp.float32), 'hl_w': jax.random.normal(ks[1], (NH, D, H), jnp.float32) * sc, 'hl_b': jax.random.normal(ks[2], (NH, D), jnp.float32) * sc, 'wq': jax.random.normal(ks[3], (NH, NE, D, D), jnp.float32) * sc, 'wk': jax.random.normal(ks[4], (NH, D, D), jnp.float32) * sc, 'wv': jax.random.normal(ks[5], (NH, D, D), jnp.float32) * sc, 'gate_w': jax.random.normal(ks[6], (NH, NE, NE * D), jnp.float32) * sc, 'gate_b': jax.random.normal(ks[7], (NH, NE), jnp.float32) * sc, 'ln_g': jnp.ones((D,), jnp.float32), 'ln_b': jnp.zeros((D,), jnp.float32), 'fc1_w': jax.random.normal(ks[8], (D, D), jnp.float32) * sc, 'fc1_b': jax.random.normal(ks[9], (D,), jnp.float32) * sc, 'fc2_w': jax.random.normal(ks[10], (D, D), jnp.float32) * sc, 'fc2_b': jax.random.normal(ks[11], (D,), jnp.float32) * sc, 'fnorm_g': jnp.ones((D,), jnp.float32), 'fnorm_b': jnp.zeros((D,), jnp.float32), 'fgate_w': jax.random.normal(ks[12], (NH, H), jnp.float32) * sc}
    _L0_ffn_all = _L0_ffn_setup()
    _L0_ffn_in = {k: v for k, v in _L0_ffn_all.items() if k in ('hl_w', 'hl_b', 'wq', 'wk', 'wv', 'gate_w', 'gate_b', 'ln_g', 'ln_b', 'fc1_w', 'fc1_b', 'fc2_w', 'fc2_b', 'fnorm_g', 'fnorm_b', 'fgate_w')}
    del _L0_ffn_all
    return {'x': x, 'adj': adj, 'L0_gnn_W': _L0_gnn_in['W'], 'L0_gnn_b': _L0_gnn_in['b'], 'L0_ffn_hl_w': _L0_ffn_in['hl_w'], 'L0_ffn_hl_b': _L0_ffn_in['hl_b'], 'L0_ffn_wq': _L0_ffn_in['wq'], 'L0_ffn_wk': _L0_ffn_in['wk'], 'L0_ffn_wv': _L0_ffn_in['wv'], 'L0_ffn_gate_w': _L0_ffn_in['gate_w'], 'L0_ffn_gate_b': _L0_ffn_in['gate_b'], 'L0_ffn_ln_g': _L0_ffn_in['ln_g'], 'L0_ffn_ln_b': _L0_ffn_in['ln_b'], 'L0_ffn_fc1_w': _L0_ffn_in['fc1_w'], 'L0_ffn_fc1_b': _L0_ffn_in['fc1_b'], 'L0_ffn_fc2_w': _L0_ffn_in['fc2_w'], 'L0_ffn_fc2_b': _L0_ffn_in['fc2_b'], 'L0_ffn_fnorm_g': _L0_ffn_in['fnorm_g'], 'L0_ffn_fnorm_b': _L0_ffn_in['fnorm_b'], 'L0_ffn_fgate_w': _L0_ffn_in['fgate_w']}

def reference(x, adj, L0_gnn_W, L0_gnn_b, L0_ffn_hl_w, L0_ffn_hl_b, L0_ffn_wq, L0_ffn_wk, L0_ffn_wv, L0_ffn_gate_w, L0_ffn_gate_b, L0_ffn_ln_g, L0_ffn_ln_b, L0_ffn_fc1_w, L0_ffn_fc1_b, L0_ffn_fc2_w, L0_ffn_fc2_b, L0_ffn_fnorm_g, L0_ffn_fnorm_b, L0_ffn_fgate_w):
    import jax
    import jax.numpy as jnp

    def _L0_gnn_ref(A, X, W, b):
        import jax, jax.numpy as jnp
        import numpy as np
        B, N, C, OUT, S = (4, 1024, 128, 128, 25)
        DENSITY = 0.008
        mask = A != 0
        neg_inf = jnp.float32(-jnp.inf)
        pri = -jnp.arange(N, dtype=jnp.float32)
        scores = jnp.where(mask, pri, neg_inf)
        vals, idx = jax.lax.top_k(scores, S)
        valid = vals > neg_inf
        feats = jax.vmap(lambda x, i: x[i])(X, idx)
        feats = jnp.where(valid[..., None], feats, neg_inf)
        agg = feats.max(axis=2)
        degree = mask.sum(axis=-1)
        agg = jnp.where((degree <= S)[..., None], jnp.maximum(agg, 0.0), agg)
        h = jnp.concatenate([X, agg], axis=-1)
        out = jax.nn.relu(jnp.einsum('bnf,fo->bno', h, W) + b)
        return out

    def _L0_ffn_ref(x, hl_w, hl_b, wq, wk, wv, gate_w, gate_b, ln_g, ln_b, fc1_w, fc1_b, fc2_w, fc2_b, fnorm_g, fnorm_b, fgate_w):
        import jax, jax.numpy as jnp
        import numpy as np
        B, S, H, NH, NE = (4, 512, 128, 4, 4)
        D = H // NH
        EPS = 1e-08

        def layernorm(x, g, b):
            m = jnp.mean(x, axis=-1, keepdims=True)
            v = jnp.mean((x - m) ** 2, axis=-1, keepdims=True)
            return (x - m) / jnp.sqrt(v + EPS) * g + b
        b, s, h = x.shape
        nh, d, _ = wk.shape
        ne = wq.shape[1]
        sx = jnp.einsum('bsh,ndh->bnsd', x, hl_w) + hl_b[None, :, None, :]
        pad = sx == 0
        q = jnp.einsum('bnsd,neod->bneso', sx, wq)
        k = jnp.einsum('bnsd,nod->bnso', sx, wk)
        v = jnp.einsum('bnsd,nod->bnso', sx, wv)
        causal = jnp.where(jnp.tril(jnp.ones((s, s), bool)), 0.0, -jnp.inf).astype(x.dtype)
        scores = jnp.einsum('bnesd,bntd->bnest', q, k) * d ** 0.5 + causal
        att = jax.nn.softmax(scores, axis=-1)
        qkv = jnp.einsum('bnest,bntd->bnesd', att, v)
        qkv = jnp.where(pad[:, :, None], 0.0, qkv)
        out = jnp.transpose(qkv, (0, 1, 3, 2, 4)).reshape(b, nh, s, ne * d)
        gs = jax.nn.softmax(jnp.einsum('bnsf,nef->bnse', out, gate_w) + gate_b[None, :, None, :], axis=-1)
        mixed = jnp.einsum('bnsed,bnse->bnsd', out.reshape(b, nh, s, ne, d), gs)
        resid = sx[jnp.arange(nh), jnp.arange(nh)]
        hn = layernorm(mixed + resid, ln_g, ln_b)
        f_n = jnp.transpose(hn, (0, 2, 1, 3)).reshape(b, s, h)
        fx = f_n.reshape(b, s, nh, d)
        pm = fx == 0
        hx = jnp.where(pm, 0.0, fx @ fc1_w.T + fc1_b)
        hx = jax.nn.relu(hx)
        hx = jnp.where(pm, 0.0, hx @ fc2_w.T + fc2_b)
        hx = layernorm(hx + fx, fnorm_g, fnorm_b)
        fout = hx.reshape(b, s, h)
        fg = jax.nn.softmax(fout @ fgate_w.T, axis=-1)
        return (fout.reshape(b, s, nh, d) * fg[..., None]).reshape(b, s, h)
    x = x + _L0_gnn_ref(adj, _layernorm(x, axis=-1), L0_gnn_W, L0_gnn_b)
    x = x + _L0_ffn_ref(_layernorm(x, axis=-1), L0_ffn_hl_w, L0_ffn_hl_b, L0_ffn_wq, L0_ffn_wk, L0_ffn_wv, L0_ffn_gate_w, L0_ffn_gate_b, L0_ffn_ln_g, L0_ffn_ln_b, L0_ffn_fc1_w, L0_ffn_fc1_b, L0_ffn_fc2_w, L0_ffn_fc2_b, L0_ffn_fnorm_g, L0_ffn_fnorm_b, L0_ffn_fgate_w)
    return x

_drawn_inputs = setup_inputs


def setup_inputs(seed=0):
    import zlib

    import numpy as np

    out = dict(_drawn_inputs(seed))
    spreads = {'L0_gnn_b': (0.0, 0.1),
     'L0_ffn_ln_g': (1.0, 0.2),
     'L0_ffn_ln_b': (0.0, 0.342),
     'L0_ffn_fnorm_g': (1.0, 0.2),
     'L0_ffn_fnorm_b': (0.0, 0.425)}
    factors = {'L0_ffn_wq': 8.0,
     'L0_ffn_wk': 8.0,
     'L0_ffn_gate_w': 8.0,
     'L0_ffn_gate_b': 45.363,
     'L0_ffn_fc1_w': 5.081,
     'L0_ffn_fc1_b': 8.0,
     'L0_ffn_fc2_w': 4.389,
     'L0_ffn_fc2_b': 4.976}
    for name, (base, spread) in spreads.items():
        noise = np.random.default_rng([zlib.crc32(name.encode()), seed]).standard_normal(out[name].shape)
        drawn = base * np.exp(spread * noise) if base else spread * noise
        out[name] = jnp.asarray(drawn.astype(out[name].dtype))
    for name, factor in factors.items():
        out[name] = (out[name] * factor).astype(out[name].dtype)
    return out
```

```python
import concourse.bass as bass
from concourse import mybir
from contextlib import ExitStack


def build(nc, x, adj, gnn_w, gnn_b, hl_t, hl_brow, hl_bcol, wq_t, wk_t, wv_t, gate_t, gate_b,
          ln_g, ln_b, fc1_t, fc1_b, fc2_t, fc2_b, fn_g, fn_b, fgate_t, out):
    F32, F32R, BF16 = mybir.dt.float32, mybir.dt.float32r, mybir.dt.bfloat16
    U32, I32 = mybir.dt.uint32, mybir.dt.int32
    ALU = mybir.AluOpType
    ACT = mybir.ActivationFunctionType
    AX = mybir.AxisListType

    B, N, C = x.shape
    P = 128
    T = N // P
    NH, NE, D = 4, 4, 32
    TOP = 25
    ROUNDS = -(-(TOP + 1) // 8)
    ZROW = B * N
    NEG = -1.0e30
    HALF = N // 2
    SCALE = float(D) ** 0.5
    EPS1, EPS2 = 1e-5, 1e-8
    LAG = 4

    rows = lambda a: a.rearrange("b (t p) c -> b p t c", p=P)
    x_v, out_v = rows(x), rows(out)
    adj_v = adj.rearrange("b (t p) m -> b t p m", p=P)
    table = nc.dram_tensor("table", (B * N + 8, C), F32, kind="Internal").ap()
    table_v = rows(table[0:B * N, :].rearrange("(b n) c -> b n c", n=N))
    x2_d = rows(nc.dram_tensor("x2_rows", (B, N, C), F32, kind="Internal").ap())
    mix_d = rows(nc.dram_tensor("mixed_rows", (B, N, C), F32, kind="Internal").ap())

    ctx = ExitStack()
    with ctx:
        sb = lambda name, shape, dt=F32: ctx.enter_context(nc.sbuf_tensor(name, shape, dt))
        sem = lambda name: ctx.enter_context(nc.semaphore(name))

        ident = sb("ident", [P, P])
        identb = sb("identb", [P, P], BF16)
        mask_qk = sb("mask_qk", [P, P], BF16)
        mask_kq = sb("mask_kq", [P, P], BF16)
        ones_row = sb("ones_row", [1, P])
        ones_den = sb("ones_den", [P, D])
        head_avg = sb("head_avg", [P, P])
        prio = sb("prio", [P, N])
        zrow = sb("zrow", [8, C])
        eps = sb("eps", [P, 2])
        ready = sb("ready", [1, 1])
        w_gnn = sb("w_gnn", [P, 2, C])
        b_gnn = sb("b_gnn", [1, C])
        w_hl = sb("w_hl", [P, NH * D])
        w_hlrep = sb("w_hlrep", [P, NH, 4, D])
        b_hlrow = sb("b_hlrow", [1, NH * D])
        b_hlrep = sb("b_hlrep", [P, NH])
        NW = NH * NE + NH + NH
        w_hi = sb("w_hi", [P, NW, D], F32R)
        w_lo = sb("w_lo", [P, NW, D], F32R)
        w_q = sb("w_q", [P, NH * NE, 3, D], F32R)
        w_k = sb("w_k", [P, NH, 3, D], F32R)
        w_v = sb("w_v", [P, NH, D], F32R)
        w_gate = sb("w_gate", [P, NH, NE])
        b_gate = sb("b_gate", [P, NH, NE])
        w_fc1 = sb("w_fc1", [P, P])
        w_fc2 = sb("w_fc2", [P, P])
        w_fg = sb("w_fg", [P, NH])
        cols = {k: sb(k + "_col", [P, 1]) for k in ("ln_g", "ln_b", "fc1_b", "fc2_b", "fn_g", "fn_b")}
        xa = sb("xa", [P, T, C])
        stats = sb("stats", [P, T, 6])
        mv = sb("mv", [P, T, 2])
        rstd = sb("rstd", [P, T])
        xn = sb("xn", [P, T, C])
        adj_t = [sb(f"adj_t{i}", [P, N], I32) for i in range(2)]
        score = sb("score", [P, N])
        prio_i = score[:, :].bitcast(I32)
        top = sb("top", [P, T, 8 * ROUNDS])
        index = sb("index", [P, T, 8 * ROUNDS], U32)
        floor = sb("floor", [P, T])
        fetched = [sb(f"fetched{i}", [P, TOP, C]) for i in range(2)]
        w_in = fetched[0][:, :, :].rearrange("p r c -> p (r c)")[:, 0:NW * D]\
            .rearrange("p (w d) -> p w d", d=D)
        agg = sb("agg", [P, T, C])
        xr = sb("xr", [P, T, C])
        xnr = sb("xnr", [P, T, C])
        agg_t = sb("agg_t", [P, N])
        xn_t = sb("xn_t", [P, N])
        x2 = sb("x2", [P, T, C])
        stats2 = sb("stats2", [P, T, 6])
        mv2 = sb("mv2", [P, T, 2])
        rstd2 = sb("rstd2", [P, T])
        xn2 = sb("xn2", [P, T, C])
        xn2_t = sb("xn2_t", [P, N])
        resid = sb("resid", [P, T, NH * D])
        sx_rep = [sb(f"sx_rep{i}", [P, N]) for i in range(2)]
        sx_st = sb("sx_st", [P, N], F32R)
        q_st = [sb(f"q_st{i}", [P, NE, N], F32R) for i in range(2)]
        k_st = [sb(f"k_st{i}", [P, N], F32R) for i in range(2)]
        v_sb = [sb(f"v_sb{i}", [P, T, D]) for i in range(2)]
        mx = sb("mx", [P, NE, T])
        mxb = sb("mxb", [P, NE, T // 2])
        mrow = sb("mrow", [NE * T, P], F32R)
        NP = 8
        probs_all = sb("probs", [P, NP * 512])
        probs = [probs_all[:, 512 * i:512 * (i + 1)] for i in range(NP)]
        o_t = sb("o_t", [P, N])
        lg = sb("lg", [P, T, NE])
        lg_s = sb("lg_s", [P, T, NE])
        lg_e = sb("lg_e", [P, T, NE])
        gs = sb("gs", [P, T, NE])
        g8 = sb("g8", [P, 3, T])
        wmix = sb("wmix", [P, N])
        mixed = sb("mixed", [P, T, NH, D])
        tm = sb("tm", [P, T, C])
        tx = sb("tx", [P, T, C])
        ty_t, tyc, tsq, trs = (probs_all[:, N * i:N * (i + 1)] for i in range(4))
        ty = xn2[:, :, :].rearrange("p t c -> p (t c)")
        tfx, tr, tz, tfo = o_t[:, :], agg_t[:, :], wmix[:, :], xn_t[:, :]
        tl = sb("tl", [P, 4, T, NH])
        t8 = sb("t8", [P, 3, T])
        tout = tm

        bank = [ctx.enter_context(nc.psum_tensor(f"bank{i}", [P, 512], F32)) for i in range(8)]
        G, MX, ST, PVO, PVD = bank[0:2], bank[2:4], bank[4:6], bank[6], bank[7]

        s_wload = sem("s_wload")
        s_wload2 = sem("s_wload2")
        s_const = sem("s_const")
        s_masks = sem("s_masks")
        s_wready = sem("s_wready")
        s_zero = sem("s_zero")
        x_in = sem("x_in")
        adj_in = [sem(f"adj_in{i}") for i in range(2)]
        table_stored = sem("table_stored")
        index_ready = sem("index_ready")
        tile_begun = sem("tile_begun")
        gather_in = [sem(f"gather_in{i}") for i in range(2)]
        fetched_read = sem("fetched_read")
        rows_in = sem("rows_in")
        x2_stored, mix_stored = sem("x2_stored"), sem("mix_stored")
        tail_in = sem("tail_in")
        out_stored = sem("out_stored")
        mrow_in = sem("mrow_in")
        go_pe, go_act, go_sp = sem("go_pe"), sem("go_act"), sem("go_sp")

        in_phase = []

        def psem(name):
            in_phase.append(sem(name))
            return in_phase[-1]

        pre_step = psem("pre_step")
        pre_act = psem("pre_act")
        rank_step = psem("rank_step")
        neigh_dve = psem("neigh_dve")
        post_pe, post_act, post_dve = psem("post_pe"), psem("post_act"), psem("post_dve")
        resid_pe, resid_dve = psem("resid_pe"), psem("resid_dve")
        job_pe = psem("job_pe")
        proj_act, proj_dve = psem("proj_act"), psem("proj_dve")
        mx_pe, mx_dve = psem("mx_pe"), psem("mx_dve")
        comb_dve = psem("comb_dve")
        mrow_act = psem("mrow_act")
        st_pe, exp_act, pv_pe = psem("st_pe"), psem("exp_act"), psem("pv_pe")
        norm_dve = psem("norm_dve")
        gate_dve, gate_act = psem("gate_dve"), psem("gate_act")
        tail_pe, tail_act, tail_dve = psem("tail_pe"), psem("tail_act"), psem("tail_dve")

        end_pe, end_act, end_sp = psem("end_pe"), psem("end_act"), psem("end_sp")
        BARRIER = [(end_pe, go_pe), (end_act, go_act), (end_sp, go_sp)]

        RANK = 2 * ROUNDS + 2
        INDEXED, FLOORED = RANK - 2, RANK - 1
        rank_at = lambda i, step: i * (RANK - 1) + min(step, RANK - 2)
        NORMED = 4
        POST_PE = ["agg0", "agg1", "xn0", "xn1", "h0", "h1", "xt0", "xt1"]
        POST_ACT = ["agg0", "agg1", "xn0", "xn1", "std", "xt0", "xt1"]
        POST_DVE = ["x20", "x21", "stat", "aggr", "rstd", "xn2"]
        at = lambda names, k: names.index(k) + 1

        NORM = 3

        PROJ = ["sx0", "sx1", "k0", "k1", "v"] + [f"q{e}{h}" for e in range(NE) for h in range(2)]
        GATE = ["lg", "row0", "row1"]
        JOBS = [(0, k) for k in PROJ] + [(0, "m")]
        for n in range(NH):
            if n + 1 < NH:
                JOBS += [(n + 1, k) for k in PROJ] + [(n + 1, "m")]
            JOBS += [(n, k) for k in GATE]
        assert len(JOBS) % 2 == 0
        P_ACT = ["sxr0", "sx0", "sxr1", "sx1", "k0", "k1", "v"] + PROJ[5:]
        P_DVE = ["sx0", "sx1", "k0", "k1"] + PROJ[5:]
        GATE_STEPS = ["lg", "max", "sub", "sum", "rec", "gs", "w0", "mix0", "w1", "mix1"]
        job_at = lambda n, k: JOBS.index((n, k)) + 1
        job_bank = lambda n, k: G[JOBS.index((n, k)) % 2]
        pact_at = lambda n, k: n * len(P_ACT) + P_ACT.index(k) + 1
        pdve_at = lambda n, k: n * len(P_DVE) + P_DVE.index(k) + 1
        gate_at = lambda n, k: n * len(GATE_STEPS) + GATE_STEPS.index(k) + 1

        def job_freed(n, k):
            if k in ("sx0", "sx1", "v"):
                return proj_act, pact_at(n, k)
            if k == "m":
                return mrow_act, n + 1
            if k in GATE:
                return gate_dve, gate_at(n, {"lg": "lg", "row0": "w0", "row1": "w1"}[k])
            return proj_dve, pdve_at(n, k)

        MAXT = [(i, kb, min(512, P * (i + 1) - 512 * kb)) for i in range(T) for kb in range(1 + i // 4)]
        STG = [(h, j, P * max(0, j - 4 * h)) for h in range(2) for j in range(4 * (h + 1))]
        NG, NT = len(STG), NE * len(STG)
        assert NT == NE * len(MAXT)
        LASTG = [max(g for g in range(NG) if STG[g][0] == h) for h in range(2)]

        T_PE = [k + h for k in ("t", "m1", "v1", "h1", "h2", "m2", "v2", "lg", "rw") for h in "01"]
        T_ACT = [k + h for k in ("t", "sq", "s1", "fx", "r1", "r2", "sz", "s2", "fo", "ex") for h in "01"]
        T_DVE = [k + h for k in ("y", "yc", "rs", "yn", "h1", "h2", "z", "zc", "rz", "zn",
                                 "lm", "ls", "su", "re", "gs", "om", "out") for h in "01"]

        def phases(e, stages, mine):

            def phase(p, kind=None):
                stages(p, kind)
                if mine is BARRIER:
                    e.drain()
                    for end, _ in BARRIER:
                        e.wait_ge(end, 1)
                    e.sem_clear(range(in_phase[0].num, in_phase[-1].num + 1))
                    for _, go in BARRIER:
                        e.drain().then_inc(go, 1)
                elif mine is not None:
                    end, go = mine
                    e.drain().then_inc(end, 1)
                    e.wait_ge(go, 1)
                    e.sem_clear(go)

            phase(-1)
            phase(0)
            phase(1)
            with e.Fori(2, LAG) as p:
                phase(p, kind=2)
            with e.Fori(LAG, B - 1) as p:
                phase(p, kind=LAG)
            phase(B - 1)
            phase(B)
            with e.Fori(B + 1, B + LAG) as p:
                phase(p, kind=B + 1)

        block = ctx.enter_context(nc.Block())

        def wait(e, s, value):
            if not isinstance(value, int) or value > 0:
                e.wait_ge(s, value)

        @block.sync
        def _(sp):
            sp.dma_start(w_gnn[:, :, :], gnn_w.rearrange("(a p) o -> p a o", p=P)).then_inc(s_wload, 16)
            sp.dma_start(w_hl[:, :], hl_t).then_inc(s_wload, 16)
            for r in range(4):
                q = slice(D * r, D * r + D)
                sp.dma_start(w_in[q, 0:16, :], wq_t).then_inc(s_wload, 16)
                sp.dma_start(w_in[q, 16:20, :], wk_t).then_inc(s_wload, 16)
                sp.dma_start(w_in[q, 20:24, :], wv_t).then_inc(s_wload, 16)
            sp.wait_ge(s_const, 1)
            sp.dma_start(table[ZROW:ZROW + 8, :], zrow[:, :]).then_inc(s_zero, 16)
            for b in range(1, B):
                sp.dma_start(table_v[b], x2[:, :, :]).then_inc(s_zero, 16)
            for r in range(4):
                q = slice(D * r, D * r + D)
                sp.dma_start(w_fc1[q, q], fc1_t).then_inc(s_wload, 16)
                sp.dma_start(w_fc2[q, q], fc2_t).then_inc(s_wload, 16)

            def load_adj(b, i):
                if i >= 2:
                    sp.wait_ge(rank_step, rank_at(i - 2, 1))
                sp.dma_start(adj_t[i % 2][:, :], adj_v[b, i]).then_inc(adj_in[i % 2], 16)

            def phase(p, kind=None):
                k = p if kind is None else kind
                pre, post, att, tail = k < B - 1, 0 <= k < B, 1 <= k <= B, k >= LAG
                if pre:
                    sp.dma_start(xa[:, :, :], x_v[p + 1]).then_inc(x_in, 16)
                    for i in range(2):
                        load_adj(p + 1, i)
                if post:
                    sp.dma_start(xr[:, :, :], x_v[p]).then_inc(rows_in, 16)
                    wait(sp, table_stored, 16 * (p + 1))
                    sp.dma_start(xnr[:, :, :], table_v[p]).then_inc(rows_in, 16)
                if tail:
                    b = p - LAG
                    if not pre:
                        wait(sp, out_stored, 16 * b)
                    wait(sp, mix_stored, 16 * (b + 1))
                    wait(sp, x2_stored, 16 * (b + 1))
                    sp.dma_start(tm[:, :, :], mix_d[b]).then_inc(tail_in, 16)
                    sp.dma_start(tx[:, :, :], x2_d[b]).then_inc(tail_in, 16)
                if tail:
                    wait(sp, tail_dve, at(T_DVE, "out1"))
                    sp.dma_start(out_v[b], tout[:, :, :]).then_inc(out_stored, 16)
                    if pre:
                        wait(sp, out_stored, 16 * (b + 1))
                if pre:
                    if k == 0:
                        sp.wait_ge(s_zero, 16 * B)
                    wait(sp, pre_step, NORMED)
                    sp.dma_start(table_v[p + 1], xn[:, :, :]).then_inc(table_stored, 16)
                for n in range(NH + 1):
                    if pre and n < 3:
                        for i in (2 * n + 2, 2 * n + 3):
                            load_adj(p + 1, i)
                    if n < NH and att:
                        wait(sp, mrow_act, n + 1)
                        sp.dma_start(q_st[n % 2][96:97, :, :].bitcast(F32)
                                     .rearrange("a e (t c) -> a (e t) c", c=P),
                                     mrow[:, :].bitcast(F32)).then_inc(mrow_in, 16)
                if att:
                    wait(sp, gate_dve, gate_at(NH - 1, "mix1"))
                    sp.dma_start(mix_d[p - 1], mixed[:, :, :, :].rearrange("p t n d -> p t (n d)"))\
                      .then_inc(mix_stored, 16)
                if post:
                    wait(sp, post_dve, at(POST_DVE, "x21"))
                    sp.dma_start(x2_d[p], x2[:, :, :]).then_inc(x2_stored, 16)

            phases(sp, phase, BARRIER[2])
            sp.wait_ge(out_stored, 16 * B)

        @block.gpsimd
        def _(pool):
            pool.memset(zrow[:, :], 0.0)
            pool.memset(x2[:, :, :], 0.0)
            pool.memset(w_fc1[:, :], 0.0)
            pool.memset(w_fc2[:, :], 0.0).then_inc(s_const, 1)
            pool.memset(ident[:, :], 0.0)
            pool.memset(identb[:, :], 0.0)
            pool.memset(mask_qk[:, :], 0.0)
            pool.memset(mask_kq[:, :], 0.0)
            pool.memset(ones_row[:, :], 1.0)
            pool.memset(eps[:, 0:1], EPS1)
            pool.memset(eps[:, 1:2], EPS2)
            pool.memset(ones_den[:, :], 1.0)
            pool.memset(head_avg[:, :], 0.0).then_inc(s_const, 1)
            pool.wait_ge(s_const, 2)
            for m in (ident, identb):
                pool.affine_select(out=m[:, :], in_=m[:, :], compare_op=ALU.not_equal, fill=1.0,
                                   base=0, pattern=[[-1, P]], channel_multiplier=1).then_inc(s_masks, 1)
            pool.affine_select(out=mask_qk[:, :], in_=mask_qk[:, :], compare_op=ALU.is_ge, fill=NEG,
                               base=0, pattern=[[-1, P]], channel_multiplier=1).then_inc(s_masks, 1)
            pool.affine_select(out=mask_kq[:, :], in_=mask_kq[:, :], compare_op=ALU.is_ge, fill=NEG,
                               base=0, pattern=[[1, P]], channel_multiplier=-1).then_inc(s_masks, 1)
            pool.wait_ge(s_masks, 4)
            for r in range(4):
                q = slice(D * r, D * r + D)
                pool.memset(head_avg[q, q], 1.0 / D).then_inc(s_masks, 1)
            pool.wait_ge(s_masks, 8)
            pool.iota(prio_i, pattern=[[-1, N]], base=ZROW, channel_multiplier=0)\
                .then_inc(s_const, 1)
            pool.wait_ge(s_zero, 16 * B)

            def phase(p, kind=None):
                k = p if kind is None else kind
                if not 0 <= k < B:
                    return
                pool.wait_ge(table_stored, 16 * (p + 1))
                for i in range(T):
                    pool.wait_ge(index_ready, p * T + i + 1)
                    if i >= 2 or k > 0:
                        pool.wait_ge(fetched_read, p * T + i - 1)
                    wait(pool, tile_begun, p * T + i)
                    pool.tensor_tensor(ready[:, :], zrow[0:1, 0:1], zrow[0:1, 0:1], ALU.add)\
                        .then_inc(tile_begun, 1)
                    for r in range(TOP):
                        pool.indirect_dma_start(
                            fetched[i % 2][:, r, :], None, table[:, :],
                            bass.IndirectOffsetOnAxis(ap=index[:, i, r:r + 1], axis=0))\
                            .then_inc(gather_in[i % 2], 16)

            phases(pool, phase, None)

        @block.scalar
        def _(act):
            act.dma_start(b_gnn[:, :], gnn_b).then_inc(s_wload2, 16)
            act.dma_start(b_hlrow[:, :], hl_brow).then_inc(s_wload2, 16)
            act.dma_start(w_gate[:, :, :], gate_t).then_inc(s_wload2, 16)
            act.dma_start(w_fg[:, :], fgate_t).then_inc(s_wload2, 16)
            act.dma_start(b_gate[:, :, :], gate_b.partition_broadcast(P)).then_inc(s_wload2, 16)
            for r in range(4):
                q = slice(D * r, D * r + D)
                act.dma_start(b_hlrep[q, :], hl_bcol).then_inc(s_wload2, 16)
                for name, src in (("ln_g", ln_g), ("ln_b", ln_b), ("fc1_b", fc1_b),
                                  ("fc2_b", fc2_b), ("fn_g", fn_g), ("fn_b", fn_b)):
                    act.dma_start(cols[name][q, :], src).then_inc(s_wload2, 16)
            act.wait_ge(s_wload2, 16 * (5 + 4 * 7))
            act.wait_ge(s_const, 3)

            def evac_post(b):
                for name, dst in (("agg", agg_t), ("xn", xn_t)):
                    for h in "01":
                        act.wait_ge(post_pe, at(POST_PE, name + h))
                        act.activation(dst[:, int(h) * HALF:(int(h) + 1) * HALF], G[int(h)][:, :],
                                       ACT.Copy).then_inc(post_act, 1)
                act.wait_ge(post_dve, at(POST_DVE, "aggr"))
                act.activation(rstd2[:, :], mv2[:, :, 1], ACT.Sqrt, bias=eps[:, 0:1]).then_inc(post_act, 1)
                for h in range(2):
                    act.wait_ge(post_pe, at(POST_PE, f"xt{h}"))
                    act.activation(xn2_t[:, h * HALF:(h + 1) * HALF], G[h][:, :], ACT.Copy)\
                       .then_inc(post_act, 1)

            def project(b, n):
                for h in range(2):
                    c = slice(h * HALF, (h + 1) * HALF)
                    act.wait_ge(job_pe, job_at(n, f"sx{h}"))
                    for dst in (sx_rep[n % 2], sx_st):
                        act.activation(dst[:, c], job_bank(n, f"sx{h}")[:, :], ACT.Identity,
                                       bias=b_hlrep[:, n:n + 1]).then_inc(proj_act, 1)
                for h in range(2):
                    c = slice(h * HALF, (h + 1) * HALF)
                    act.wait_ge(job_pe, job_at(n, f"k{h}"))
                    act.activation(k_st[n % 2][0:96, c], job_bank(n, f"k{h}")[0:96, :], ACT.Copy)\
                       .then_inc(proj_act, 1)
                act.wait_ge(job_pe, job_at(n, "v"))
                act.activation(v_sb[n % 2][:, :, :], job_bank(n, "v")[:, 0:T * D]
                               .rearrange("p (t d) -> p t d", d=D), ACT.Copy).then_inc(proj_act, 1)
                for e in range(NE):
                    for h in range(2):
                        c = slice(h * HALF, (h + 1) * HALF)
                        act.wait_ge(job_pe, job_at(n, f"q{e}{h}"))
                        act.activation(q_st[n % 2][0:96, e, c], job_bank(n, f"q{e}{h}")[0:96, :],
                                       ACT.Copy).then_inc(proj_act, 1)

            def max_rows(b, n, k):
                act.wait_ge(job_pe, job_at(n, "m"))
                if not (k == 1 and n == 0):
                    act.wait_ge(mrow_in, 16 * (b * NH + n))
                act.activation(mrow[:, :], job_bank(n, "m")[0:NE * T, 0:P], ACT.Copy, scale=-1.0)\
                   .then_inc(mrow_act, 1)

            def exps(b, n, k):
                for t in range(NT):
                    g, e = divmod(t, NE)
                    w = 512 - STG[g][2]
                    act.wait_ge(st_pe, n * NT + t + 1)
                    if e == 0 and n * NG + g >= 2:
                        act.wait_ge(pv_pe, n * NG + g - 1)
                    act.activation(probs[t % NP][:, 0:w], ST[t % 2][:, 0:w], ACT.Exp, scale=SCALE)\
                       .then_inc(exp_act, 1)

            def tail(b):
                h2 = lambda h: slice(int(h) * HALF, (int(h) + 1) * HALF)

                def step(name, dst, src, func, src_sem, value, **kw):
                    act.wait_ge(src_sem, value)
                    act.activation(dst, src, func, **kw).then_inc(tail_act, 1)

                for h in "01":
                    step("t", ty_t[:, h2(h)], G[int(h)][:, :], ACT.Copy, tail_pe, at(T_PE, "t" + h))
                for h in "01":
                    step("sq", tsq[:, h2(h)], tyc[:, h2(h)], ACT.Square, tail_dve, at(T_DVE, "yc" + h))
                for h in "01":
                    step("s1", trs[:, h2(h)], G[int(h)][:, :], ACT.Sqrt, tail_pe,
                         at(T_PE, "v1" + h), bias=eps[:, 1:2])
                for h in "01":
                    step("fx", tfx[:, h2(h)], ty[:, h2(h)], ACT.Identity, tail_dve,
                         at(T_DVE, "yn" + h), scale=cols["ln_g"][:, :], bias=cols["ln_b"][:, :])
                for h in "01":
                    step("r1", tr[:, h2(h)], G[int(h)][:, :], ACT.Relu, tail_pe,
                         at(T_PE, "h1" + h), bias=cols["fc1_b"][:, :])
                for h in "01":
                    step("r2", tr[:, h2(h)], G[int(h)][:, :], ACT.Identity, tail_pe,
                         at(T_PE, "h2" + h), bias=cols["fc2_b"][:, :])
                for h in "01":
                    step("sz", tsq[:, h2(h)], tyc[:, h2(h)], ACT.Square, tail_dve, at(T_DVE, "zc" + h))
                for h in "01":
                    step("s2", trs[:, h2(h)], G[int(h)][:, :], ACT.Sqrt, tail_pe,
                         at(T_PE, "v2" + h), bias=eps[:, 1:2])
                for h in "01":
                    step("fo", tfo[:, h2(h)], ty[:, h2(h)], ACT.Identity, tail_dve,
                         at(T_DVE, "zn" + h), scale=cols["fn_g"][:, :], bias=cols["fn_b"][:, :])
                for h in range(2):
                    ts = slice(4 * h, 4 * h + 4)
                    step("ex", tl[:, 1, ts, :], tl[:, 0, ts, :], ACT.Exp, tail_dve,
                         at(T_DVE, f"ls{h}"))

            def phase(p, kind=None):
                k = p if kind is None else kind
                if k >= LAG:
                    tail(p - LAG)
                if k < B - 1:
                    act.wait_ge(pre_step, 2)
                    act.activation(rstd[:, :], mv[:, :, 1], ACT.Sqrt, bias=eps[:, 0:1])\
                       .then_inc(pre_act, 1)
                if 1 <= k <= B:
                    b = p - 1
                    project(b, 0)
                    max_rows(b, 0, k)
                    for n in range(NH):
                        if n + 1 < NH:
                            project(b, n + 1)
                        exps(b, n, k)
                        if n + 1 < NH:
                            max_rows(b, n + 1, k)
                        act.wait_ge(gate_dve, gate_at(n, "sub"))
                        act.activation(lg_e[:, :, :], lg_s[:, :, :], ACT.Exp).then_inc(gate_act, 1)
                if 0 <= k < B:
                    evac_post(p)

            phases(act, phase, BARRIER[1])

        @block.tensor
        def _(pe):
            mm = pe.matmul
            pe.wait_ge(s_wload, 16 * (2 + 12 + 8))
            pe.wait_ge(s_wload2, 16 * (5 + 4 * 7))
            pe.wait_ge(s_const, 3)
            pe.wait_ge(s_wready, 1)

            def job(b, n, k, first):
                j = JOBS.index((n, k))
                if j >= 2:
                    pe.wait_ge(*job_freed(*JOBS[j - 2]))
                return job_bank(n, k)

            def project(b, n, first):
                for h in range(2):
                    ps = job(b, n, f"sx{h}", first)
                    mm(ps[:, :], w_hlrep[:, n, :, :].rearrange("p r d -> p (r d)"),
                       xn2_t[:, h * HALF:(h + 1) * HALF], start=True, stop=True).then_inc(job_pe, 1)
                for h in range(2):
                    ps = job(b, n, f"k{h}", first)
                    pe.wait_ge(proj_dve, pdve_at(n, f"sx{h}"))
                    mm(ps[0:96, :], w_k[:, n, :, :].rearrange("p r d -> p (r d)"),
                       sx_st[:, h * HALF:(h + 1) * HALF], start=True, stop=True).then_inc(job_pe, 1)
                ps = job(b, n, "v", first)
                for t in range(T):
                    m = mm(ps[:, t * D:(t + 1) * D], sx_st[:, t * P:(t + 1) * P], w_v[:, n, :],
                           start=True, stop=True)
                m.then_inc(job_pe, 1)
                for e in range(NE):
                    for h in range(2):
                        ps = job(b, n, f"q{e}{h}", first)
                        mm(ps[0:96, :], w_q[:, n * NE + e, :, :].rearrange("p r d -> p (r d)"),
                           sx_st[:, h * HALF:(h + 1) * HALF], start=True, stop=True)\
                            .then_inc(job_pe, 1)

            def max_tile(b, n, t, k):
                e, m = divmod(t, len(MAXT))
                i, kb, w = MAXT[m]
                g = n * NT + t
                if t == 0:
                    pe.wait_ge(proj_dve, pdve_at(n, f"q{NE - 1}1"))
                if g >= 2:
                    pe.wait_ge(mx_dve, g - 1)
                ps = MX[t % 2]
                diag = P * i // 512 == kb
                last = mm(ps[:, 0:w], q_st[n % 2][0:96, e, i * P:(i + 1) * P],
                          k_st[n % 2][0:96, 512 * kb:512 * kb + w], start=True, stop=not diag)
                if diag:
                    last = mm(ps[:, w - P:w], identb[:, :], mask_qk[:, :], start=False, stop=True)
                last.then_inc(mx_pe, 1)

            def score_tile(b, n, t, k):
                g, e = divmod(t, NE)
                h, j, off = STG[g]
                w = 512 - off
                if t == 0:
                    pe.wait_ge(mrow_in, 16 * (b * NH + n + 1))
                u = n * NT + t
                if u >= 2:
                    pe.wait_ge(exp_act, u - 1)
                ps = ST[t % 2]
                diag = j >= 4 * h
                last = mm(ps[:, 0:w], k_st[n % 2][0:97, j * P:(j + 1) * P],
                          q_st[n % 2][0:97, e, h * HALF + off:(h + 1) * HALF], start=True, stop=not diag)
                if diag:
                    last = mm(ps[:, 0:P], identb[:, :], mask_kq[:, :], start=False, stop=True)
                last.then_inc(st_pe, 1)

            def values(b, n, g, k):
                h, j, off = STG[g]
                pe.wait_ge(exp_act, n * NT + NE * (g + 1))
                if j == 0 and n + h > 0:
                    pe.wait_ge(norm_dve, NORM * (n * 2 + h))
                for e in range(NE):
                    pr = probs[(NE * g + e) % NP][:, 0:512 - off]
                    q = slice(D * e, D * e + D)
                    mm(PVO[q, off:512], v_sb[n % 2][:, j, :], pr, start=j == 0, stop=g == LASTG[h])
                for e in range(NE):
                    pr = probs[(NE * g + e) % NP][:, 0:512 - off]
                    q = slice(D * e, D * e + D)
                    last = mm(PVD[q, off:512], ones_den[:, :], pr, start=j == 0, stop=g == LASTG[h])
                last.then_inc(pv_pe, 1)

            def max_rows(b, n, first):
                pe.wait_ge(comb_dve, n + 1)
                ps = job(b, n, "m", first)
                pe.transpose(ps[0:NE * T, 0:P], mx[:, :, :].rearrange("p e t -> p (e t)"), ident[:, :])\
                  .then_inc(job_pe, 1)

            def gate(b, n, first):
                pe.wait_ge(norm_dve, NORM * (n * 2 + 2))
                ps = job(b, n, "lg", first)
                for t in range(T):
                    m = mm(ps[:, t * NE:(t + 1) * NE], o_t[:, t * P:(t + 1) * P], w_gate[:, n, :],
                           start=True, stop=True)
                m.then_inc(job_pe, 1)
                for h in range(2):
                    ps = job(b, n, f"row{h}", first)
                    for t in range(4):
                        m = pe.transpose(ps[:, t * P:(t + 1) * P],
                                         o_t[:, h * HALF + t * P:h * HALF + (t + 1) * P], ident[:, :])
                    m.then_inc(job_pe, 1)

            def attention(b, k):
                first = False
                project(b, 0, first)
                for t in range(NT):
                    max_tile(b, 0, t, k)
                max_rows(b, 0, first)
                for n in range(NH):
                    if n + 1 < NH:
                        project(b, n + 1, first)
                    for t in range(NT):
                        score_tile(b, n, t, k)
                        if n + 1 < NH:
                            max_tile(b, n + 1, t, k)
                        if t % NE == NE - 1 and t >= 2 * NE - 1:
                            values(b, n, t // NE - 1, k)
                    values(b, n, NG - 1, k)
                    if n + 1 < NH:
                        max_rows(b, n + 1, first)
                    gate(b, n, first)

            def post(b, k, resids):
                if k >= 1:
                    pe.wait_ge(gate_dve, gate_at(NH - 1, "w1"))
                pe.wait_ge(neigh_dve, T)
                for h in range(2):
                    for t in range(4):
                        m = pe.transpose(G[h][:, t * P:(t + 1) * P], agg[:, 4 * h + t, :], ident[:, :])
                    m.then_inc(post_pe, 1)
                pe.wait_ge(rows_in, 32 * (b + 1))
                for h in range(2):
                    pe.wait_ge(post_act, at(POST_ACT, f"agg{h}"))
                    for t in range(4):
                        m = pe.transpose(G[h][:, t * P:(t + 1) * P], xnr[:, 4 * h + t, :], ident[:, :])
                    m.then_inc(post_pe, 1)
                for h in range(2):
                    pe.wait_ge(post_act, at(POST_ACT, f"xn{h}"))
                    for t in range(4):
                        c = slice((4 * h + t) * P, (4 * h + t + 1) * P)
                        ps = G[h][:, t * P:(t + 1) * P]
                        mm(ps, xn_t[:, c], w_gnn[:, 0, :], start=True, stop=False)
                        mm(ps, agg_t[:, c], w_gnn[:, 1, :], start=False, stop=False)
                        m = mm(ps, ones_row[:, :], b_gnn[:, :], start=False, stop=True)
                    m.then_inc(post_pe, 1)
                pe.wait_ge(post_dve, at(POST_DVE, "xn2"))
                for h in range(2):
                    for t in range(4):
                        m = pe.transpose(G[h][:, t * P:(t + 1) * P], xn2[:, 4 * h + t, :], ident[:, :])
                    m.then_inc(post_pe, 1)
                if resids:
                    for h in range(2):
                        pe.wait_ge(post_act, at(POST_ACT, f"xt{h}"))
                        for t in range(4):
                            c = slice((4 * h + t) * P, (4 * h + t + 1) * P)
                            ps = G[h][:, t * P:(t + 1) * P]
                            mm(ps, xn2_t[:, c], w_hl[:, :], start=True, stop=False)
                            m = mm(ps, ones_row[:, :], b_hlrow[:, :], start=False, stop=True)
                        m.then_inc(resid_pe, 1)

            def tail(b, k):
                c2 = lambda h: slice(int(h) * HALF, (int(h) + 1) * HALF)
                for h in "01":
                    pe.wait_ge(tail_dve, at(T_DVE, "y" + h))
                    for t in range(4):
                        col = (4 * int(h) + t) * P
                        m = pe.transpose(G[int(h)][:, t * P:(t + 1) * P], ty[:, col:col + P], ident[:, :])
                    m.then_inc(tail_pe, 1)
                for src, w, s, names, key in (
                        (ty_t, head_avg, tail_act, T_ACT, "t"), (tsq, head_avg, tail_act, T_ACT, "sq"),
                        (tfx, w_fc1, tail_act, T_ACT, "fx"), (tz, w_fc2, tail_dve, T_DVE, "h1"),
                        (tz, head_avg, tail_dve, T_DVE, "z"), (tsq, head_avg, tail_act, T_ACT, "sz")):
                    for h in "01":
                        pe.wait_ge(s, at(names, key + h))
                        mm(G[int(h)][:, :], w[:, :], src[:, c2(h)], start=True, stop=True)\
                            .then_inc(tail_pe, 1)
                for h in "01":
                    pe.wait_ge(tail_act, at(T_ACT, "fo" + h))
                    for t in range(4):
                        col = (4 * int(h) + t) * P
                        m = mm(G[int(h)][:, t * NH:(t + 1) * NH], tfo[:, col:col + P], w_fg[:, :],
                               start=True, stop=True)
                    m.then_inc(tail_pe, 1)
                for h in "01":
                    pe.wait_ge(tail_dve, at(T_DVE, "ls" + h))
                    for t in range(4):
                        col = (4 * int(h) + t) * P
                        m = pe.transpose(G[int(h)][:, t * P:(t + 1) * P], tfo[:, col:col + P], ident[:, :])
                    m.then_inc(tail_pe, 1)
                pe.wait_ge(tail_dve, at(T_DVE, "om1"))

            def phase(p, kind=None):
                k = p if kind is None else kind
                if k >= LAG:
                    tail(p - LAG, k)
                if 1 <= k <= B:
                    attention(p - 1, k)
                if 0 <= k < B:
                    post(p, k, k < LAG)

            phases(pe, phase, BARRIER[0])

        @block.vector
        def _(dve):
            dve.wait_ge(s_wload, 16 * (2 + 12 + 8))
            dve.wait_ge(s_const, 3)
            dve.tensor_copy(prio[:, :], prio_i)
            for r in range(4):
                dve.tensor_copy(w_hlrep[:, :, r, :], w_hl[:, :].rearrange("p (n d) -> p n d", d=D))
            for i in range(2):
                dve.memset(k_st[i][96:97, :].bitcast(F32), 1.0)
            dve.tensor_copy(w_hi[:, :, :], w_in[:, :, :]).then_inc(s_wready, 1)
            dve.wait_ge(s_wready, 1)
            dve.tensor_tensor(w_lo[:, :, :], w_in[:, :, :], w_hi[:, :, :].bitcast(F32), ALU.subtract)\
               .then_inc(s_wready, 1)
            dve.wait_ge(s_wready, 2)
            for r in range(4):
                q = slice(D * r, D * r + D)
                src = (w_hi if r % 2 == 0 else w_lo)
                for c in range(3):
                    dve.tensor_copy(w_q[q, :, c, :], src[q, 0:16, :].bitcast(F32))
                    dve.tensor_copy(w_k[q, :, c, :], src[q, 16:20, :].bitcast(F32))
                last = dve.tensor_copy(w_v[q, :, :], src[q, 20:24, :].bitcast(F32))
            last.then_inc(s_wready, 1)

            def normalise(src, st, m, rs, dst, s, base, std_act, std_value):
                for t in range(T):
                    last = dve.bn_stats(st[:, t, :], src[:, t, :])
                last.then_inc(s, 1)
                dve.wait_ge(s, base + 1)
                for t in range(T):
                    last = dve.bn_aggr(m[:, t, :], st[:, t, :])
                last.then_inc(s, 1)
                dve.wait_ge(std_act, std_value)
                dve.reciprocal(rs[:, :], rs[:, :]).then_inc(s, 1)
                dve.wait_ge(s, base + 3)
                for t in range(T):
                    last = dve.tensor_scalar(dst[:, t, :], src[:, t, :], m[:, t, 0:1], rs[:, t:t + 1],
                                             ALU.subtract, ALU.mult)
                last.then_inc(s, 1)

            def pre(b, k):
                dve.wait_ge(x_in, 16 * (b + 1))
                if k >= 0:
                    dve.wait_ge(table_stored, 16 * b)
                normalise(xa, stats, mv, rstd, xn, pre_step, 0, pre_act, 1)
                if k >= 0:
                    dve.tensor_scalar(prio[:, :], prio[:, :], float(-N), None, ALU.add)\
                       .then_inc(pre_step, 1)

            def rank(b, i, step):
                if step == 0:
                    dve.wait_ge(adj_in[i % 2], (b * (T // 2) + i // 2 + 1) * 16)
                    if i > 0:
                        dve.wait_ge(rank_step, rank_at(i, 0))
                    elif not (isinstance(b, int) and b == 0):
                        dve.wait_ge(pre_step, NORMED + 1)
                    dve.scalar_tensor_tensor(score[:, :], adj_t[i % 2][:, :], 0.0, prio[:, :],
                                             ALU.not_equal, ALU.mult).then_inc(rank_step, 1)
                    return
                dve.wait_ge(rank_step, rank_at(i, step))
                r, what = divmod(step - 1, 2)
                eight = top[:, i, 8 * r:8 * r + 8] if r < ROUNDS else None
                if step == INDEXED:
                    dve.tensor_scalar(index[:, i, :], top[:, i, :], -1.0, float(ZROW),
                                      ALU.mult, ALU.add).then_inc(index_ready, 1)
                elif step == FLOORED:
                    dve.tensor_scalar(floor[:, i:i + 1], top[:, i, TOP:TOP + 1], 0.0, NEG,
                                      ALU.is_gt, ALU.mult).then_inc(rank_step, 1)
                elif what == 0:
                    dve.max(eight, score[:, :]).then_inc(rank_step, 1)
                else:
                    dve.match_replace(score[:, :], eight, score[:, :], 0.0).then_inc(rank_step, 1)

            def neighbours(b, i, step):
                if step == 0:
                    dve.wait_ge(gather_in[i % 2], (b * (T // 2) + i // 2 + 1) * 16 * TOP)
                    dve.tensor_reduce(agg[:, i, :], fetched[i % 2][:, :, :].rearrange("p r c -> p c r"),
                                      AX.X, ALU.max).then_inc(fetched_read, 1)
                else:
                    dve.wait_ge(fetched_read, b * T + i + 1)
                    dve.tensor_scalar(agg[:, i, :], agg[:, i, :], floor[:, i:i + 1], None, ALU.max)\
                       .then_inc(neigh_dve, 1)

            STEPS = 2 + RANK

            def gnn_step(p, k, s):
                i, r = divmod(s, STEPS)
                if r < 2:
                    if 0 <= k < B:
                        neighbours(p, i, r)
                elif k < B - 1:
                    rank(p + 1, i, r - 2)

            def post(b, k, resids):
                for h in range(2):
                    dve.wait_ge(post_pe, at(POST_PE, f"h{h}"))
                    if h == 0:
                        dve.wait_ge(rows_in, 32 * (b + 1))
                        if k >= 1:
                            dve.wait_ge(x2_stored, 16 * b)
                    ts = slice(4 * h, 4 * h + 4)
                    dve.scalar_tensor_tensor(x2[:, ts, :], G[h][:, :].rearrange("p (t c) -> p t c", c=C),
                                             0.0, xr[:, ts, :], ALU.max, ALU.add).then_inc(post_dve, 1)
                dve.wait_ge(post_dve, at(POST_DVE, "x21"))
                normalise(x2, stats2, mv2, rstd2, xn2, post_dve, at(POST_DVE, "x21"),
                          post_act, at(POST_ACT, "std"))
                if resids:
                    for h in range(2):
                        dve.wait_ge(resid_pe, h + 1)
                        ts = slice(4 * h, 4 * h + 4)
                        src = G[h][:, :].rearrange("p (t c) -> p t c", c=C)
                        if isinstance(b, int):
                            c = slice(b * D, (b + 1) * D)
                        else:
                            c = bass.ds(b * D, D)
                        dve.tensor_copy(resid[:, ts, c], src[:, :, c]).then_inc(resid_dve, 1)

            def project(b, n):
                for h in range(2):
                    c = slice(h * HALF, (h + 1) * HALF)
                    dve.wait_ge(proj_act, pact_at(n, f"sx{h}"))
                    dve.tensor_tensor(sx_st[64:128, c], sx_rep[n % 2][64:128, c],
                                      sx_st[64:128, c].bitcast(F32), ALU.subtract).then_inc(proj_dve, 1)
                for h in range(2):
                    c = slice(h * HALF, (h + 1) * HALF)
                    dve.wait_ge(proj_act, pact_at(n, f"k{h}"))
                    dve.tensor_tensor(k_st[n % 2][32:64, c], job_bank(n, f"k{h}")[32:64, :],
                                      k_st[n % 2][32:64, c].bitcast(F32), ALU.subtract)\
                       .then_inc(proj_dve, 1)
                for e in range(NE):
                    for h in range(2):
                        c = slice(h * HALF, (h + 1) * HALF)
                        dve.wait_ge(proj_act, pact_at(n, f"q{e}{h}"))
                        dve.tensor_tensor(q_st[n % 2][64:96, e, c], job_bank(n, f"q{e}{h}")[64:96, :],
                                          q_st[n % 2][64:96, e, c].bitcast(F32), ALU.subtract)\
                           .then_inc(proj_dve, 1)

            def max_tile(b, n, t):
                e, m = divmod(t, len(MAXT))
                i, kb, w = MAXT[m]
                dve.wait_ge(mx_pe, n * NT + t + 1)
                dst = mx[:, e, i:i + 1] if kb == 0 else mxb[:, e, i - 4:i - 3]
                dve.tensor_reduce(dst, MX[t % 2][:, 0:w], AX.X, ALU.max).then_inc(mx_dve, 1)

            def combine(b, n):
                dve.wait_ge(mx_dve, (n + 1) * NT)
                dve.tensor_tensor(mx[:, :, 4:8], mx[:, :, 4:8], mxb[:, :, :], ALU.max)\
                   .then_inc(comb_dve, 1)

            def norm(b, n, h):
                c = slice(h * HALF, (h + 1) * HALF)
                dve.wait_ge(pv_pe, n * NG + LASTG[h] + 1)
                dve.reciprocal(o_t[:, c], PVD[:, :]).then_inc(norm_dve, 1)
                dve.wait_ge(norm_dve, NORM * (n * 2 + h) + 1)
                dve.scalar_tensor_tensor(o_t[:, c], sx_rep[n % 2][:, c], 0.0, o_t[:, c],
                                         ALU.not_equal, ALU.mult).then_inc(norm_dve, 1)
                dve.wait_ge(norm_dve, NORM * (n * 2 + h) + 2)
                dve.tensor_tensor(o_t[:, c], o_t[:, c], PVO[:, :], ALU.mult).then_inc(norm_dve, 1)

            def over(small, like):
                return small.unsqueeze(len(small.shape)).broadcast_to(like)

            def softmax4(src, work, part, exped, dst, s, a_sem, a_value, at_step, keys):
                t = src.shape[1]
                dve.tensor_reduce(part[0], src, AX.X, ALU.max).then_inc(s, 1)
                dve.wait_ge(s, at_step(keys[0]))
                dve.tensor_tensor(work, src, over(part[0], [P, t, 4]), ALU.subtract).then_inc(s, 1)
                dve.wait_ge(a_sem, a_value)
                dve.tensor_reduce(part[1], exped, AX.X, ALU.add).then_inc(s, 1)
                dve.wait_ge(s, at_step(keys[2]))
                dve.reciprocal(part[2], part[1]).then_inc(s, 1)
                dve.wait_ge(s, at_step(keys[3]))
                dve.tensor_tensor(dst, exped, over(part[2], [P, t, 4]), ALU.mult).then_inc(s, 1)
                dve.wait_ge(s, at_step(keys[4]))

            def gate(b, n, k):
                step = lambda key: gate_at(n, key)
                dve.wait_ge(job_pe, job_at(n, "lg"))
                dve.tensor_tensor(lg[:, :, :], job_bank(n, "lg")[:, 0:T * NE]
                                  .rearrange("p (t e) -> p t e", e=NE),
                                  b_gate[:, n:n + 1, :].broadcast_to([P, T, NE]), ALU.add)\
                   .then_inc(gate_dve, 1)
                dve.wait_ge(gate_dve, step("lg"))
                softmax4(lg[:, :, :], lg_s[:, :, :], [g8[:, j, :] for j in range(3)], lg_e[:, :, :],
                         gs[:, :, :], gate_dve, gate_act, n + 1, step,
                         ["max", "sub", "sum", "rec", "gs"])
                if n == 0 and k != 1:
                    dve.wait_ge(mix_stored, 16 * b)
                for h in range(2):
                    dve.wait_ge(job_pe, job_at(n, f"row{h}"))
                    ts = slice(4 * h, 4 * h + 4)
                    c = slice(h * HALF, (h + 1) * HALF)
                    dve.tensor_tensor(wmix[:, c].rearrange("p (t d) -> p t d", d=D),
                                      job_bank(n, f"row{h}")[:, :].rearrange("p (t d) -> p t d", d=D),
                                      over(gs[:, ts, :].rearrange("p t e -> p (t e)"), [P, 16, D]),
                                      ALU.mult).then_inc(gate_dve, 1)
                    dve.wait_ge(gate_dve, step(f"w{h}"))
                    dve.tensor_reduce(mixed[:, ts, n, :], wmix[:, c]
                                      .rearrange("p (t e d) -> p t d e", e=NE, d=D),
                                      AX.X, ALU.add).then_inc(gate_dve, 1)

            def attention(p, k):
                b = p - 1
                step = 0
                project(b, 0)
                for t in range(NT):
                    max_tile(b, 0, t)
                    if t % 2:
                        gnn_step(p, k, step)
                        step += 1
                combine(b, 0)
                for n in range(NH):
                    if n + 1 < NH:
                        project(b, n + 1)
                    for t in range(NT):
                        if n + 1 < NH:
                            max_tile(b, n + 1, t)
                            if t % 2:
                                gnn_step(p, k, step)
                                step += 1
                        if t == NE * (LASTG[0] + 2):
                            norm(b, n, 0)
                    if n + 1 < NH:
                        combine(b, n + 1)
                    norm(b, n, 1)
                    gate(b, n, k)
                assert step == STEPS * T

            def tail(b, k):
                c2 = lambda h: slice(int(h) * HALF, (int(h) + 1) * HALF)

                def did(i):
                    i.then_inc(tail_dve, 1)

                def mine(key):
                    dve.wait_ge(tail_dve, at(T_DVE, key))

                dve.wait_ge(tail_in, 32 * (b + 1))
                r3 = lambda t_, h: t_[:, c2(h)].rearrange("p (t c) -> p t c", c=C)
                for h in "01":
                    ts = slice(4 * int(h), 4 * int(h) + 4)
                    did(dve.tensor_tensor(r3(ty, h), tm[:, ts, :], resid[:, ts, :], ALU.add))

                def layernorm(src, pkey, skey, z):
                    for h in "01":
                        dve.wait_ge(tail_pe, at(T_PE, pkey + h))
                        if z:
                            mine("z" + h)
                        did(dve.tensor_tensor(tyc[:, c2(h)], src[:, c2(h)], G[int(h)][:, :], ALU.subtract))
                    for h in "01":
                        dve.wait_ge(tail_act, at(T_ACT, skey + h))
                        did(dve.reciprocal(trs[:, c2(h)], trs[:, c2(h)]))
                    for h in "01":
                        mine(("rz" if z else "rs") + h)
                        did(dve.tensor_tensor(ty[:, c2(h)], tyc[:, c2(h)], trs[:, c2(h)], ALU.mult))

                layernorm(ty_t, "m1", "s1", False)
                for h in "01":
                    dve.wait_ge(tail_act, at(T_ACT, "r1" + h))
                    did(dve.scalar_tensor_tensor(tz[:, c2(h)], tfx[:, c2(h)], 0.0, tr[:, c2(h)],
                                                 ALU.not_equal, ALU.mult))
                for h in "01":
                    dve.wait_ge(tail_act, at(T_ACT, "r2" + h))
                    did(dve.scalar_tensor_tensor(tz[:, c2(h)], tfx[:, c2(h)], 0.0, tr[:, c2(h)],
                                                 ALU.not_equal, ALU.mult))
                for h in "01":
                    mine("h2" + h)
                    did(dve.tensor_tensor(tz[:, c2(h)], tz[:, c2(h)], tfx[:, c2(h)], ALU.add))
                layernorm(tz, "m2", "s2", True)
                psl = lambda h: G[h][:, 0:16].rearrange("p (t n) -> p t n", n=NH)
                hs = [slice(0, 4), slice(4, 8)]
                for h in range(2):
                    dve.wait_ge(tail_pe, at(T_PE, f"lg{h}"))
                    did(dve.tensor_reduce(t8[:, 0, hs[h]], psl(h), AX.X, ALU.max))
                for h in range(2):
                    mine(f"lm{h}")
                    did(dve.tensor_tensor(tl[:, 0, hs[h], :], psl(h), over(t8[:, 0, hs[h]], [P, 4, NH]),
                                          ALU.subtract))
                for h in range(2):
                    dve.wait_ge(tail_act, at(T_ACT, f"ex{h}"))
                    did(dve.tensor_reduce(t8[:, 1, hs[h]], tl[:, 1, hs[h], :], AX.X, ALU.add))
                for h in range(2):
                    mine(f"su{h}")
                    did(dve.reciprocal(t8[:, 2, hs[h]], t8[:, 1, hs[h]]))
                for h in range(2):
                    mine(f"re{h}")
                    did(dve.tensor_tensor(tl[:, 2, hs[h], :], tl[:, 1, hs[h], :],
                                          over(t8[:, 2, hs[h]], [P, 4, NH]), ALU.mult))
                r4 = lambda a: a.rearrange("p (g d) -> p g d", d=D)
                for h in range(2):
                    dve.wait_ge(tail_pe, at(T_PE, f"rw{h}"))
                    mine(f"gs{h}")
                    did(dve.tensor_tensor(r4(ty[:, c2(h)]), r4(G[h][:, :]),
                                          over(tl[:, 2, hs[h], :].rearrange("p t n -> p (t n)"), [P, 16, D]),
                                          ALU.mult))
                for h in range(2):
                    mine(f"om{h}")
                    did(dve.tensor_tensor(tout[:, hs[h], :], r3(ty, h), tx[:, hs[h], :], ALU.add))

            def phase(p, kind=None):
                k = p if kind is None else kind
                if k >= LAG:
                    tail(p - LAG, k)
                if k < B - 1:
                    pre(p + 1, k)
                if 1 <= k <= B:
                    attention(p, k)
                else:
                    for s in range(STEPS * T):
                        gnn_step(p, k, s)
                if 0 <= k < B:
                    post(p, k, k < LAG)

            phases(dve, phase, BARRIER)


def kernel(x, adj, L0_gnn_W, L0_gnn_b, L0_ffn_hl_w, L0_ffn_hl_b, L0_ffn_wq, L0_ffn_wk, L0_ffn_wv,
           L0_ffn_gate_w, L0_ffn_gate_b, L0_ffn_ln_g, L0_ffn_ln_b, L0_ffn_fc1_w, L0_ffn_fc1_b,
           L0_ffn_fc2_w, L0_ffn_fc2_b, L0_ffn_fnorm_g, L0_ffn_fnorm_b, L0_ffn_fgate_w):
    import numpy as np
    import concourse.bacc as bacc
    from concourse.bass_utils import run_bass_kernel_spmd

    a = lambda v, *shape: np.ascontiguousarray(np.asarray(v).reshape(shape))
    t = lambda v, *axes: np.ascontiguousarray(np.asarray(v).transpose(axes))
    nh, d, h = np.asarray(L0_ffn_hl_w).shape
    ne = np.asarray(L0_ffn_wq).shape[1]
    ins = {
        "x": np.asarray(x), "adj": np.asarray(adj), "gnn_w": np.asarray(L0_gnn_W),
        "gnn_b": a(L0_gnn_b, 1, h),
        "hl_t": t(L0_ffn_hl_w, 2, 0, 1).reshape(h, nh * d),
        "hl_brow": a(L0_ffn_hl_b, 1, nh * d), "hl_bcol": t(L0_ffn_hl_b, 1, 0),
        "wq_t": t(L0_ffn_wq, 3, 0, 1, 2).reshape(d, nh * ne, d),
        "wk_t": t(L0_ffn_wk, 2, 0, 1), "wv_t": t(L0_ffn_wv, 2, 0, 1),
        "gate_t": t(L0_ffn_gate_w, 2, 0, 1), "gate_b": np.asarray(L0_ffn_gate_b),
        "ln_g": a(L0_ffn_ln_g, d, 1), "ln_b": a(L0_ffn_ln_b, d, 1),
        "fc1_t": t(L0_ffn_fc1_w, 1, 0), "fc1_b": a(L0_ffn_fc1_b, d, 1),
        "fc2_t": t(L0_ffn_fc2_w, 1, 0), "fc2_b": a(L0_ffn_fc2_b, d, 1),
        "fn_g": a(L0_ffn_fnorm_g, d, 1), "fn_b": a(L0_ffn_fnorm_b, d, 1),
        "fgate_t": t(L0_ffn_fgate_w, 1, 0),
    }
    nc = bacc.Bacc("TRN2", target_bir_lowering=False, num_devices=1)
    args = [nc.dram_tensor(f"in_{k}", v.shape, mybir.dt.from_np(v.dtype), kind="ExternalInput").ap()
            for k, v in ins.items()]
    out = nc.dram_tensor("out", ins["x"].shape, mybir.dt.float32, kind="ExternalOutput").ap()
    build(nc, *args, out)
    r = run_bass_kernel_spmd(nc, [{f"in_{k}": v for k, v in ins.items()}], core_ids=[0])
    return r.results[0]["out"]
```

```python
import concourse.bass as bass
from concourse import mybir
from contextlib import ExitStack


def build(nc, x, adj, gnn_w, gnn_b, hl_t, hl_brow, hl_bcol, wq_t, wk_t, wv_t, gate_t, gate_b,
          ln_g, ln_b, fc1_t, fc1_b, fc2_t, fc2_b, fn_g, fn_b, fgate_t, out):
    F32, F32R, BF16 = mybir.dt.float32, mybir.dt.float32r, mybir.dt.bfloat16
    U32, I32 = mybir.dt.uint32, mybir.dt.int32
    ALU = mybir.AluOpType
    ACT = mybir.ActivationFunctionType
    AX = mybir.AxisListType

    B, N, C = x.shape
    P = 128
    T = N // P
    NH, NE, D = 4, 4, 32
    TOP = 25
    ROUNDS = -(-(TOP + 1) // 8)
    ZROW = B * N
    NEG = -1.0e30
    HALF = N // 2
    SCALE = float(D) ** 0.5
    EPS1, EPS2 = 1e-5, 1e-8
    WARM = 8
    LAG = 4

    rows = lambda a: a.rearrange("b (t p) c -> b p t c", p=P)
    x_v, out_v = rows(x), rows(out)
    adj_v = adj.rearrange("b (t p) m -> b t p m", p=P)
    table = nc.dram_tensor("table", (B * N + 8, C), F32, kind="Internal").ap()
    table_v = rows(table[0:B * N, :].rearrange("(b n) c -> b n c", n=N))
    x2_d = rows(nc.dram_tensor("x2_rows", (B, N, C), F32, kind="Internal").ap())
    mix_d = rows(nc.dram_tensor("mixed_rows", (B, N, C), F32, kind="Internal").ap())

    ctx = ExitStack()
    with ctx:
        sb = lambda name, shape, dt=F32: ctx.enter_context(nc.sbuf_tensor(name, shape, dt))
        sem = lambda name: ctx.enter_context(nc.semaphore(name))

        ident = sb("ident", [P, P])
        identb = sb("identb", [P, P], BF16)
        mask_qk = sb("mask_qk", [P, P], BF16)
        mask_kq = sb("mask_kq", [P, P], BF16)
        ones_row = sb("ones_row", [1, P])
        ones_den = sb("ones_den", [P, D])
        head_avg = sb("head_avg", [P, P])
        prio = sb("prio", [P, N])
        zrow = sb("zrow", [8, C])
        eps = sb("eps", [P, 2])
        ready = sb("ready", [1, 1])
        w_gnn = sb("w_gnn", [P, 2, C])
        b_gnn = sb("b_gnn", [1, C])
        w_hl = sb("w_hl", [P, NH * D])
        w_hlrep = sb("w_hlrep", [P, NH, 4, D])
        b_hlrow = sb("b_hlrow", [1, NH * D])
        b_hlrep = sb("b_hlrep", [P, NH])
        NW = NH * NE + NH + NH
        w_hi = sb("w_hi", [P, NW, D], F32R)
        w_lo = sb("w_lo", [P, NW, D], F32R)
        w_q = sb("w_q", [P, NH * NE, 3, D], F32R)
        w_k = sb("w_k", [P, NH, 3, D], F32R)
        w_v = sb("w_v", [P, NH, D], F32R)
        w_gate = sb("w_gate", [P, NH, NE])
        w_gatex = sb("w_gatex", [P, NH, NE, NE])
        pick = sb("pick", [P, NE])
        b_gate = sb("b_gate", [P, NH, NE])
        w_fc1 = sb("w_fc1", [P, P])
        w_fc2 = sb("w_fc2", [P, P])
        w_fg = sb("w_fg", [P, NH])
        cols = {k: sb(k + "_col", [P, 1]) for k in ("ln_g", "ln_b", "fc1_b", "fc2_b", "fn_g", "fn_b")}
        xa = sb("xa", [P, T, C])
        stats = sb("stats", [P, T, 6])
        mv = sb("mv", [P, T, 2])
        rstd = sb("rstd", [P, T])
        xn = sb("xn", [P, T, C])
        adj_t = [sb(f"adj_t{i}", [P, N], I32) for i in range(2)]
        score = sb("score", [P, N])
        prio_i = score[:, :].bitcast(I32)
        top = sb("top", [P, T, 8 * ROUNDS])
        index = sb("index", [P, T, 8 * ROUNDS], U32)
        floor = sb("floor", [P, T])
        fetched = [sb(f"fetched{i}", [P, TOP, C]) for i in range(2)]
        w_in = fetched[0][:, :, :].rearrange("p r c -> p (r c)")[:, 0:NW * D]\
            .rearrange("p (w d) -> p w d", d=D)
        agg = sb("agg", [P, T, C])
        xr = sb("xr", [P, T, C])
        xnr = sb("xnr", [P, T, C])
        agg_t = sb("agg_t", [P, N])
        xn_t = sb("xn_t", [P, N])
        x2 = sb("x2", [P, T, C])
        stats2 = sb("stats2", [P, T, 6])
        mv2 = sb("mv2", [P, T, 2])
        rstd2 = sb("rstd2", [P, T])
        xn2 = sb("xn2", [P, T, C])
        xn2_t = sb("xn2_t", [P, N])
        resid = sb("resid", [P, T, NH * D])
        sx_rep = [sb(f"sx_rep{i}", [P, N]) for i in range(2)]
        sx_st = sb("sx_st", [P, N], F32R)
        q_st = [sb(f"q_st{i}", [P, NE, N], F32R) for i in range(2)]
        k_st = [sb(f"k_st{i}", [P, N], F32R) for i in range(2)]
        v_sb = [sb(f"v_sb{i}", [P, T, D]) for i in range(2)]
        mx = sb("mx", [P, NE, T])
        mxb = sb("mxb", [P, NE, T // 2])
        mrow = sb("mrow", [NE * T, P], F32R)
        NP = 8
        probs_all = sb("probs", [P, NP * 512])
        probs = [probs_all[:, 512 * i:512 * (i + 1)] for i in range(NP)]
        o_t = sb("o_t", [P, N])
        den_t = sb("den_t", [P, N])
        lg = sb("lg", [P, T, NE])
        part_lg = sb("part_lg", [P, T, NE, NE])
        rden = sb("rden", [P, T, NE])
        lg_s = sb("lg_s", [P, T, NE])
        lg_e = sb("lg_e", [P, T, NE])
        gs = sb("gs", [P, T, NE])
        g8 = sb("g8", [P, 3, T])
        wmix = sb("wmix", [P, N])
        mixed = sb("mixed", [P, T, NH, D])
        tm = sb("tm", [P, T, C])
        tx = sb("tx", [P, T, C])
        ty_t, tyc, tsq, trs = (probs_all[:, N * i:N * (i + 1)] for i in range(4))
        ty = xn2[:, :, :].rearrange("p t c -> p (t c)")
        tfx, tr, tz, tfo = o_t[:, :], agg_t[:, :], wmix[:, :], xn_t[:, :]
        tl = sb("tl", [P, 4, T, NH])
        t8 = sb("t8", [P, 3, T])
        tout = tm

        bank = [ctx.enter_context(nc.psum_tensor(f"bank{i}", [P, 512], F32)) for i in range(8)]
        G, MX, ST, PVO, PVD = bank[0:2], bank[2:4], bank[4:6], bank[6], bank[7]

        s_wload = sem("s_wload")
        s_wload2 = sem("s_wload2")
        s_const = sem("s_const")
        s_masks = sem("s_masks")
        s_wready = sem("s_wready")
        s_zero = sem("s_zero")
        x_in = sem("x_in")
        adj_in = [sem(f"adj_in{i}") for i in range(2)]
        table_stored = sem("table_stored")
        index_ready = sem("index_ready")
        tile_begun = sem("tile_begun")
        gather_in = [sem(f"gather_in{i}") for i in range(2)]
        fetched_read = sem("fetched_read")
        rows_in = sem("rows_in")
        x2_stored, mix_stored = sem("x2_stored"), sem("mix_stored")
        tail_in = sem("tail_in")
        out_stored = sem("out_stored")
        mrow_in = sem("mrow_in")
        go_pe, go_act, go_sp = sem("go_pe"), sem("go_act"), sem("go_sp")

        in_phase = []

        def psem(name):
            in_phase.append(sem(name))
            return in_phase[-1]

        pre_step = psem("pre_step")
        pre_act = psem("pre_act")
        rank_step = psem("rank_step")
        neigh_dve = psem("neigh_dve")
        post_pe, post_act, post_dve = psem("post_pe"), psem("post_act"), psem("post_dve")
        resid_pe, resid_dve = psem("resid_pe"), psem("resid_dve")
        job_pe = psem("job_pe")
        proj_act, proj_dve = psem("proj_act"), psem("proj_dve")
        mx_pe, mx_dve = psem("mx_pe"), psem("mx_dve")
        comb_dve = psem("comb_dve")
        mrow_act = psem("mrow_act")
        st_pe, exp_act, pv_pe = psem("st_pe"), psem("exp_act"), psem("pv_pe")
        out_dve, den_act = psem("out_dve"), psem("den_act")
        gate_dve, gate_act = psem("gate_dve"), psem("gate_act")
        tail_pe, tail_act, tail_dve = psem("tail_pe"), psem("tail_act"), psem("tail_dve")

        end_pe, end_act, end_sp = psem("end_pe"), psem("end_act"), psem("end_sp")
        BARRIER = [(end_pe, go_pe), (end_act, go_act), (end_sp, go_sp)]

        RANK = 2 * ROUNDS + 2
        INDEXED, FLOORED = RANK - 2, RANK - 1
        rank_at = lambda i, step: i * (RANK - 1) + min(step, RANK - 2)
        NORMED = 4
        POST_PE = ["agg0", "agg1", "xn0", "xn1", "h0", "h1", "xt0", "xt1"]
        POST_ACT = ["agg0", "agg1", "xn0", "xn1", "std", "xt0", "xt1"]
        POST_DVE = ["x20", "x21", "stat", "aggr", "rstd", "xn2"]
        at = lambda names, k: names.index(k) + 1

        LG = NE * NE + NE

        PROJ = ["sx0", "sx1", "k0", "k1", "v"] + [f"q{e}{h}" for e in range(NE) for h in range(2)]
        GATE = ["lg", "row0", "row1"]
        JOBS = [(0, k) for k in PROJ] + [(1, k) for k in PROJ] + [(0, "m")]
        JOB_AT = {-1: {5 * (i // 2) + 1 + 2 * (i % 2): [(1, k)] for i, k in enumerate(PROJ)}}
        GATE_AT = {"lg": 2, "row0": 4, "row1": 5}
        MAX_FROM = {0: 0}
        for n in range(NH):
            JOB_AT[n] = {GATE_AT[k]: [(n - 1, k)] for k in GATE} if n else {}
            if 0 < n < NH - 1:
                JOB_AT[n][0] = [(n + 1, "sx0"), (n + 1, "sx1")]
                for i, k in enumerate(PROJ[2:]):
                    JOB_AT[n][8 + i] = [(n + 1, k)]
                MAX_FROM[n] = 8 + len(PROJ)
            for slot in sorted(JOB_AT[n]):
                JOBS += JOB_AT[n][slot]
            if n + 1 < NH:
                JOBS += [(n + 1, "m")]
        JOBS += [(NH - 1, k) for k in GATE]
        assert len(JOBS) % 2 == 0 and len(set(JOBS)) == len(JOBS)
        P_ACT = ["sxr0", "sx0", "sxr1", "sx1", "k0", "k1", "v"] + PROJ[5:]
        P_DVE = ["sx0", "sx1", "k0", "k1"] + PROJ[5:]
        GATE_STEPS = ["rd", "pl", "sl", "lg", "max", "sub", "sum", "rec", "gs", "gr",
                      "w0", "mix0", "w1", "mix1"]
        job_at = lambda n, k: JOBS.index((n, k)) + 1
        job_bank = lambda n, k: G[JOBS.index((n, k)) % 2]
        pact_at = lambda n, k: n * len(P_ACT) + P_ACT.index(k) + 1
        pdve_at = lambda n, k: n * len(P_DVE) + P_DVE.index(k) + 1
        gate_at = lambda n, k: n * len(GATE_STEPS) + GATE_STEPS.index(k) + 1

        def job_freed(n, k):
            if k in ("sx0", "sx1", "v"):
                return proj_act, pact_at(n, k)
            if k == "m":
                return mrow_act, n + 1
            if k in GATE:
                return gate_dve, gate_at(n, {"lg": "pl", "row0": "w0", "row1": "w1"}[k])
            return proj_dve, pdve_at(n, k)

        MAXT = [(i, kb, min(512, P * (i + 1) - 512 * kb)) for i in range(T) for kb in range(1 + i // 4)]
        STG = [(h, j, P * max(0, j - 4 * h)) for h in range(2) for j in range(4 * (h + 1))]
        NG, NT = len(STG), NE * len(STG)
        assert NT == NE * len(MAXT)
        max_tiles = lambda n, t: range(*(max(0, NT * (u - MAX_FROM[n]) // (NT - MAX_FROM[n]))
                                         for u in (t, t + 1))) if n in MAX_FROM else ()
        LASTG = [max(g for g in range(NG) if STG[g][0] == h) for h in range(2)]

        T_PE = [k + h for k in ("t", "m1", "v1", "h1", "h2", "m2", "v2", "lg", "rw") for h in "01"]
        T_ACT = [k + h for k in ("t", "sq", "l1", "s1", "fx", "r1", "r2", "sz", "l2", "s2", "fo", "ex")
                 for h in "01"]
        T_DVE = [k + h for k in ("y", "yc", "yn", "h1", "h2", "z", "zc", "zn",
                                 "lm", "ls", "su", "re", "gs", "om", "out") for h in "01"]

        TAIL_PE = ["t", "m1", "v1", "h1", "h2", "m2", "v2", "lg", "rw"]
        TAIL_DVE = ["y", None, "yc", "yn", "h1", "h2", "zc", "zn", "soft", "out"]
        TAIL_EVERY = 5
        assert TAIL_EVERY * (len(TAIL_DVE) - 1) < NT
        POST_PE_AT = {1: "agg", 3: "xn", 5: "h", 8: "xt", 10: "resid"}
        POST_ACT_AT = {2: "agg", 4: "xn", 7: "std", 9: "xt"}
        POST_DVE_AT = {6: "x2", 8: "xn2", 11: "resid"}
        TAIL_ACT_AT = {4: ["t"], 10: ["sq"], 14: ["l1", "s1"], 15: ["fx"], 19: ["r1"], 24: ["r2"],
                       30: ["sz"], 34: ["l2", "s2"], 35: ["fo"], 40: ["ex"]}

        tile_max = lambda i: [("max", i, s) for s in range(2)]
        tile_rank = lambda i: [("rank", i, s) for s in range(RANK)]
        GNN = {-1: tile_max(0) + tile_rank(0) + tile_max(1),
               0: tile_max(2) + tile_rank(1) + tile_max(3) + tile_rank(2),
               1: tile_max(4) + tile_rank(3) + tile_max(5),
               2: tile_max(6) + tile_rank(4) + tile_max(7),
               3: tile_rank(5) + tile_rank(6) + tile_rank(7)}
        SPAN = {-1: NT, 0: NT, 1: 40, 2: 40, 3: NT}
        gnn_steps = lambda w, t: GNN[w][len(GNN[w]) * t // SPAN[w]:len(GNN[w]) * (t + 1) // SPAN[w]]
        ADJ_LOADS = [(2,), (3, 4), (5,), (6,), (7,)]

        def phases(e, stages, mine):

            def phase(p, kind=None):
                stages(p, kind)
                if mine is BARRIER:
                    e.drain()
                    for end, _ in BARRIER:
                        e.wait_ge(end, 1)
                    e.sem_clear(range(in_phase[0].num, in_phase[-1].num + 1))
                    for _, go in BARRIER:
                        e.drain().then_inc(go, 1)
                elif mine is not None:
                    end, go = mine
                    e.drain().then_inc(end, 1)
                    e.wait_ge(go, 1)
                    e.sem_clear(go)

            phase(-1)
            phase(0)
            phase(1)
            with e.Fori(2, LAG) as p:
                phase(p, kind=2)
            with e.Fori(LAG, B - 1) as p:
                phase(p, kind=LAG)
            phase(B - 1)
            phase(B)
            with e.Fori(B + 1, B + LAG) as p:
                phase(p, kind=B + 1)

        block = ctx.enter_context(nc.Block())

        def wait(e, s, value):
            if not isinstance(value, int) or value > 0:
                e.wait_ge(s, value)

        @block.sync
        def _(sp):
            sp.dma_start(w_gnn[:, :, :], gnn_w.rearrange("(a p) o -> p a o", p=P)).then_inc(s_wload, 16)
            sp.dma_start(w_hl[:, :], hl_t).then_inc(s_wload, 16)
            for r in range(4):
                q = slice(D * r, D * r + D)
                sp.dma_start(w_in[q, 0:16, :], wq_t).then_inc(s_wload, 16)
                sp.dma_start(w_in[q, 16:20, :], wk_t).then_inc(s_wload, 16)
                sp.dma_start(w_in[q, 20:24, :], wv_t).then_inc(s_wload, 16)
            sp.wait_ge(s_const, 1)
            sp.dma_start(table[ZROW:ZROW + 8, :], zrow[:, :]).then_inc(s_zero, 16)
            for b in range(1, B):
                sp.dma_start(table_v[b], x2[:, :, :]).then_inc(s_zero, 16)
            for r in range(4):
                q = slice(D * r, D * r + D)
                sp.dma_start(w_fc1[q, q], fc1_t).then_inc(s_wload, 16)
                sp.dma_start(w_fc2[q, q], fc2_t).then_inc(s_wload, 16)

            def load_adj(b, i):
                if i >= 2:
                    sp.wait_ge(rank_step, rank_at(i - 2, 1))
                sp.dma_start(adj_t[i % 2][:, :], adj_v[b, i]).then_inc(adj_in[i % 2], 16)

            def phase(p, kind=None):
                k = p if kind is None else kind
                pre, post, att, tail = k < B - 1, 0 <= k < B, 1 <= k <= B, k >= LAG
                if pre:
                    sp.dma_start(xa[:, :, :], x_v[p + 1]).then_inc(x_in, 16)
                    for i in range(2):
                        load_adj(p + 1, i)
                if post:
                    sp.dma_start(xr[:, :, :], x_v[p]).then_inc(rows_in, 16)
                    wait(sp, table_stored, 16 * (p + 1))
                    sp.dma_start(xnr[:, :, :], table_v[p]).then_inc(rows_in, 16)
                if tail:
                    b = p - LAG
                    if not pre:
                        wait(sp, out_stored, 16 * b)
                    wait(sp, mix_stored, 16 * (b + 1))
                    wait(sp, x2_stored, 16 * (b + 1))
                    sp.dma_start(tm[:, :, :], mix_d[b]).then_inc(tail_in, 16)
                    sp.dma_start(tx[:, :, :], x2_d[b]).then_inc(tail_in, 16)
                if tail:
                    wait(sp, tail_dve, at(T_DVE, "out1"))
                    sp.dma_start(out_v[b], tout[:, :, :]).then_inc(out_stored, 16)
                if pre:
                    if k == 0:
                        sp.wait_ge(s_zero, 16 * B)
                    wait(sp, pre_step, NORMED)
                    sp.dma_start(table_v[p + 1], xn[:, :, :]).then_inc(table_stored, 16)
                for n in range(NH + 1):
                    if pre:
                        for i in ADJ_LOADS[n]:
                            load_adj(p + 1, i)
                    if n < NH and att:
                        wait(sp, mrow_act, n + 1)
                        sp.dma_start(q_st[n % 2][96:97, :, :].bitcast(F32)
                                     .rearrange("a e (t c) -> a (e t) c", c=P),
                                     mrow[:, :].bitcast(F32)).then_inc(mrow_in, 16)
                if tail and pre:
                    wait(sp, out_stored, 16 * (p - LAG + 1))
                if att:
                    wait(sp, gate_dve, gate_at(NH - 1, "mix1"))
                    sp.dma_start(mix_d[p - 1], mixed[:, :, :, :].rearrange("p t n d -> p t (n d)"))\
                      .then_inc(mix_stored, 16)
                if post:
                    wait(sp, post_dve, at(POST_DVE, "x21"))
                    sp.dma_start(x2_d[p], x2[:, :, :]).then_inc(x2_stored, 16)

            phases(sp, phase, BARRIER[2])
            sp.wait_ge(out_stored, 16 * B)

        @block.gpsimd
        def _(pool):
            pool.memset(zrow[:, :], 0.0)
            pool.memset(x2[:, :, :], 0.0)
            pool.memset(w_fc1[:, :], 0.0)
            pool.memset(w_fc2[:, :], 0.0).then_inc(s_const, 1)
            pool.memset(ident[:, :], 0.0)
            pool.memset(identb[:, :], 0.0)
            pool.memset(mask_qk[:, :], 0.0)
            pool.memset(mask_kq[:, :], 0.0)
            pool.memset(ones_row[:, :], 1.0)
            pool.memset(eps[:, 0:1], EPS1)
            pool.memset(eps[:, 1:2], EPS2)
            pool.memset(ones_den[:, :], 1.0)
            pool.memset(pick[:, :], 0.0)
            pool.memset(w_gatex[:, :, :, :], 0.0)
            pool.memset(head_avg[:, :], 0.0).then_inc(s_const, 1)
            pool.wait_ge(s_const, 2)
            for m in (ident, identb):
                pool.affine_select(out=m[:, :], in_=m[:, :], compare_op=ALU.not_equal, fill=1.0,
                                   base=0, pattern=[[-1, P]], channel_multiplier=1).then_inc(s_masks, 1)
            pool.affine_select(out=pick[:, :], in_=pick[:, :], compare_op=ALU.not_equal, fill=1.0,
                               base=0, pattern=[[-D, NE]], channel_multiplier=1).then_inc(s_masks, 1)
            pool.affine_select(out=mask_qk[:, :], in_=mask_qk[:, :], compare_op=ALU.is_ge, fill=NEG,
                               base=0, pattern=[[-1, P]], channel_multiplier=1).then_inc(s_masks, 1)
            pool.affine_select(out=mask_kq[:, :], in_=mask_kq[:, :], compare_op=ALU.is_ge, fill=NEG,
                               base=0, pattern=[[1, P]], channel_multiplier=-1).then_inc(s_masks, 1)
            pool.wait_ge(s_masks, 5)
            for r in range(4):
                q = slice(D * r, D * r + D)
                pool.memset(head_avg[q, q], 1.0 / D).then_inc(s_masks, 1)
            pool.wait_ge(s_masks, 9)
            pool.iota(prio_i, pattern=[[-1, N]], base=ZROW, channel_multiplier=0)\
                .then_inc(s_const, 1)
            for i in range(2):
                pool.wait_ge(s_const, 3 + i)
                pool.memset(q_st[i][96:128, :, :].bitcast(F32), 0.0).then_inc(s_const, 1)
            pool.wait_ge(s_const, 5)
            pool.wait_ge(s_zero, 16 * B)

            def phase(p, kind=None):
                k = p if kind is None else kind
                if not 0 <= k < B:
                    return
                pool.wait_ge(table_stored, 16 * (p + 1))
                for i in range(T):
                    pool.wait_ge(index_ready, p * T + i + 1)
                    if i >= 2 or k > 0:
                        pool.wait_ge(fetched_read, p * T + i - 1)
                    wait(pool, tile_begun, p * T + i)
                    pool.tensor_tensor(ready[:, :], zrow[0:1, 0:1], zrow[0:1, 0:1], ALU.add)\
                        .then_inc(tile_begun, 1)
                    for r in range(TOP):
                        pool.indirect_dma_start(
                            fetched[i % 2][:, r, :], None, table[:, :],
                            bass.IndirectOffsetOnAxis(ap=index[:, i, r:r + 1], axis=0))\
                            .then_inc(gather_in[i % 2], 16)

            phases(pool, phase, None)

        @block.scalar
        def _(act):
            act.dma_start(b_gnn[:, :], gnn_b).then_inc(s_wload2, 16)
            act.dma_start(b_hlrow[:, :], hl_brow).then_inc(s_wload2, 16)
            act.dma_start(w_gate[:, :, :], gate_t).then_inc(s_wload2, 16)
            act.dma_start(w_fg[:, :], fgate_t).then_inc(s_wload2, 16)
            act.dma_start(b_gate[:, :, :], gate_b.partition_broadcast(P)).then_inc(s_wload2, 16)
            for r in range(4):
                q = slice(D * r, D * r + D)
                act.dma_start(b_hlrep[q, :], hl_bcol).then_inc(s_wload2, 16)
                for name, src in (("ln_g", ln_g), ("ln_b", ln_b), ("fc1_b", fc1_b),
                                  ("fc2_b", fc2_b), ("fn_g", fn_g), ("fn_b", fn_b)):
                    act.dma_start(cols[name][q, :], src).then_inc(s_wload2, 16)
            act.wait_ge(s_wload2, 16 * (5 + 4 * 7))
            act.wait_ge(s_const, 3)

            def post(stage):
                if stage == "std":
                    act.wait_ge(post_dve, at(POST_DVE, "aggr"))
                    act.activation(rstd2[:, :], mv2[:, :, 1], ACT.Sqrt, bias=eps[:, 0:1])\
                       .then_inc(post_act, 1)
                    return
                dst = {"agg": agg_t, "xn": xn_t, "xt": xn2_t}[stage]
                for h in range(2):
                    act.wait_ge(post_pe, at(POST_PE, f"{stage}{h}"))
                    act.activation(dst[:, h * HALF:(h + 1) * HALF], MX[h][:, :], ACT.Copy)\
                       .then_inc(post_act, 1)

            def project(n, key):
                act.wait_ge(job_pe, job_at(n, key))
                ps = job_bank(n, key)
                h = 0 if key == "v" else int(key[-1])
                c = slice(h * HALF, (h + 1) * HALF)
                if key[:2] == "sx":
                    if n >= 2:
                        act.wait_ge(out_dve, 2 * (n - 1))
                    for dst in (sx_rep[n % 2], sx_st):
                        act.activation(dst[:, c], ps[:, :], ACT.Identity, bias=b_hlrep[:, n:n + 1])\
                           .then_inc(proj_act, 1)
                elif key == "v":
                    act.activation(v_sb[n % 2][:, :, :], ps[:, 0:T * D]
                                   .rearrange("p (t d) -> p t d", d=D), ACT.Copy).then_inc(proj_act, 1)
                else:
                    dst = k_st[n % 2][0:96, c] if key[0] == "k" else q_st[n % 2][0:96, int(key[1]), c]
                    act.activation(dst, ps[0:96, :], ACT.Copy).then_inc(proj_act, 1)

            def gate(n):
                act.wait_ge(gate_dve, gate_at(n, "sub"))
                act.activation(lg_e[:, :, :], lg_s[:, :, :], ACT.Exp).then_inc(gate_act, 1)

            def max_rows(b, n, k):
                act.wait_ge(job_pe, job_at(n, "m"))
                if not (k == 1 and n == 0):
                    act.wait_ge(mrow_in, 16 * (b * NH + n))
                act.activation(mrow[:, :], job_bank(n, "m")[0:NE * T, 0:P], ACT.Copy, scale=-1.0)\
                   .then_inc(mrow_act, 1)

            def denominators(n, h):
                act.wait_ge(pv_pe, n * NG + LASTG[h] + 1)
                if h == 0 and n > 0:
                    act.wait_ge(job_pe, job_at(n - 1, "lg"))
                act.activation(den_t[:, h * HALF:(h + 1) * HALF], PVD[:, :], ACT.Copy)\
                   .then_inc(den_act, 1)

            def exps(b, n, k):
                for t in range(NT):
                    g, e = divmod(t, NE)
                    for m, key in JOB_AT[n].get(t, []):
                        if m == n + 1:
                            project(m, key)
                        elif key == "row1":
                            gate(m)
                    if e == 0 and n == NH - 1 and k < B and g in POST_ACT_AT:
                        post(POST_ACT_AT[g])
                    if t == NE * (LASTG[0] + 2):
                        denominators(n, 0)
                    w = 512 - STG[g][2]
                    act.wait_ge(st_pe, n * NT + t + 1)
                    if e == 0 and n * NG + g >= 2:
                        act.wait_ge(pv_pe, n * NG + g - 1)
                    act.activation(probs[t % NP][:, 0:w], ST[t % 2][:, 0:w], ACT.Exp, scale=SCALE)\
                       .then_inc(exp_act, 1)
                denominators(n, 1)

            def tail(stage):
                dst, src, func, s, names, key, kw = {
                    "t": (ty_t, None, ACT.Copy, tail_pe, T_PE, "t", {}),
                    "sq": (tsq, tyc, ACT.Square, tail_dve, T_DVE, "yc", {}),
                    "l1": (trs, None, ACT.Ln, tail_pe, T_PE, "v1", {"bias": eps[:, 1:2]}),
                    "s1": (trs, trs, ACT.Exp, tail_act, T_ACT, "l1", {"scale": -0.5}),
                    "fx": (tfx, ty, ACT.Identity, tail_dve, T_DVE, "yn",
                           {"scale": cols["ln_g"][:, :], "bias": cols["ln_b"][:, :]}),
                    "r1": (tr, None, ACT.Relu, tail_pe, T_PE, "h1", {"bias": cols["fc1_b"][:, :]}),
                    "r2": (tr, None, ACT.Identity, tail_pe, T_PE, "h2", {"bias": cols["fc2_b"][:, :]}),
                    "sz": (tsq, tyc, ACT.Square, tail_dve, T_DVE, "zc", {}),
                    "l2": (trs, None, ACT.Ln, tail_pe, T_PE, "v2", {"bias": eps[:, 1:2]}),
                    "s2": (trs, trs, ACT.Exp, tail_act, T_ACT, "l2", {"scale": -0.5}),
                    "fo": (tfo, ty, ACT.Identity, tail_dve, T_DVE, "zn",
                           {"scale": cols["fn_g"][:, :], "bias": cols["fn_b"][:, :]}),
                    "ex": (None, None, ACT.Exp, tail_dve, T_DVE, "ls", {}),
                }[stage]
                for h in range(2):
                    c, ts = slice(h * HALF, (h + 1) * HALF), slice(4 * h, 4 * h + 4)
                    act.wait_ge(s, at(names, f"{key}{h}"))
                    if stage == "ex":
                        act.activation(tl[:, 1, ts, :], tl[:, 0, ts, :], func).then_inc(tail_act, 1)
                    else:
                        act.activation(dst[:, c], ST[h][:, :] if src is None else src[:, c], func, **kw)\
                           .then_inc(tail_act, 1)

            def phase(p, kind=None):
                k = p if kind is None else kind
                att = 1 <= k <= B
                if att:
                    for key in PROJ:
                        project(0, key)
                if k < B - 1:
                    act.wait_ge(pre_step, 2)
                    act.activation(rstd[:, :], mv[:, :, 1], ACT.Sqrt, bias=eps[:, 0:1])\
                       .then_inc(pre_act, 1)
                for t in range(NT):
                    if k >= LAG:
                        for stage in TAIL_ACT_AT.get(t, []):
                            tail(stage)
                    if att:
                        for n, key in JOB_AT[-1].get(t, []):
                            project(n, key)
                if att:
                    b = p - 1
                    max_rows(b, 0, k)
                    for n in range(NH):
                        exps(b, n, k)
                        if n + 1 < NH:
                            max_rows(b, n + 1, k)
                    gate(NH - 1)
                elif k == 0:
                    for stage in POST_ACT_AT.values():
                        post(stage)

            phases(act, phase, BARRIER[1])

        @block.tensor
        def _(pe):
            mm = pe.matmul
            pe.wait_ge(s_wload, 16 * (2 + 12 + 8))
            pe.wait_ge(s_wload2, 16 * (5 + 4 * 7))
            pe.wait_ge(s_const, 5)
            pe.wait_ge(s_wready, 5)

            def job(b, n, k, first):
                j = JOBS.index((n, k))
                if j >= 2:
                    pe.wait_ge(*job_freed(*JOBS[j - 2]))
                return job_bank(n, k)

            def project(b, n, key):
                ps = job(b, n, key, False)
                h = 0 if key == "v" else int(key[-1])
                c = slice(h * HALF, (h + 1) * HALF)
                if key[:2] == "sx":
                    m = mm(ps[:, :], w_hlrep[:, n, :, :].rearrange("p r d -> p (r d)"), xn2_t[:, c],
                           start=True, stop=True)
                elif key == "v":
                    for t in range(T):
                        m = mm(ps[:, t * D:(t + 1) * D], sx_st[:, t * P:(t + 1) * P], w_v[:, n, :],
                               start=True, stop=True)
                else:
                    if key[0] == "k":
                        pe.wait_ge(proj_dve, pdve_at(n, f"sx{h}"))
                    w = w_k[:, n, :, :] if key[0] == "k" else w_q[:, n * NE + int(key[1]), :, :]
                    m = mm(ps[0:96, :], w.rearrange("p r d -> p (r d)"), sx_st[:, c],
                           start=True, stop=True)
                m.then_inc(job_pe, 1)

            def max_tile(b, n, t, k):
                e, m = divmod(t, len(MAXT))
                i, kb, w = MAXT[m]
                g = n * NT + t
                if t == 0:
                    pe.wait_ge(proj_dve, pdve_at(n, f"q{NE - 1}1"))
                if g >= 2:
                    pe.wait_ge(mx_dve, g - 1)
                ps = MX[t % 2]
                diag = P * i // 512 == kb
                last = mm(ps[:, 0:w], q_st[n % 2][0:96, e, i * P:(i + 1) * P],
                          k_st[n % 2][0:96, 512 * kb:512 * kb + w], start=True, stop=not diag)
                if diag:
                    last = mm(ps[:, w - P:w], identb[:, :], mask_qk[:, :], start=False, stop=True)
                last.then_inc(mx_pe, 1)

            def score_tile(b, n, t, k):
                g, e = divmod(t, NE)
                h, j, off = STG[g]
                w = 512 - off
                if t == 0:
                    pe.wait_ge(mrow_in, 16 * (b * NH + n + 1))
                u = n * NT + t
                if u >= 2:
                    pe.wait_ge(exp_act, u - 1)
                ps = ST[t % 2]
                diag = j >= 4 * h
                last = mm(ps[:, 0:w], k_st[n % 2][:, j * P:(j + 1) * P],
                          q_st[n % 2][:, e, h * HALF + off:(h + 1) * HALF], start=True, stop=not diag)
                if diag:
                    last = mm(ps[:, 0:P], identb[:, :], mask_kq[:, :], start=False, stop=True)
                last.then_inc(st_pe, 1)

            def values(n, g):
                h, j, off = STG[g]
                pe.wait_ge(exp_act, n * NT + NE * (g + 1))
                if j == 0 and n + h > 0:
                    pe.wait_ge(out_dve, n * 2 + h)
                for e in range(NE):
                    mm(PVO[D * e:D * e + D, off:512], v_sb[n % 2][:, j, :],
                       probs[(NE * g + e) % NP][:, 0:512 - off], start=j == 0, stop=g == LASTG[h])

            def sums(n, g):
                h, j, off = STG[g]
                if j == 0 and n + h > 0:
                    pe.wait_ge(den_act, n * 2 + h)
                for e in range(NE):
                    last = mm(PVD[D * e:D * e + D, off:512], ones_den[:, :],
                              probs[(NE * g + e) % NP][:, 0:512 - off], start=j == 0, stop=g == LASTG[h])
                last.then_inc(pv_pe, 1)

            def max_rows(b, n, first):
                pe.wait_ge(comb_dve, n + 1)
                ps = job(b, n, "m", first)
                pe.transpose(ps[0:NE * T, 0:P], mx[:, :, :].rearrange("p e t -> p (e t)"), ident[:, :])\
                  .then_inc(job_pe, 1)

            def gate(b, n, key):
                if key == "lg":
                    pe.wait_ge(out_dve, n * 2 + 2)
                    pe.wait_ge(den_act, n * 2 + 2)
                    ps = job(b, n, key, False)
                    for t in range(T):
                        q = LG * t
                        mm(ps[:, q:q + NE * NE], o_t[:, t * P:(t + 1) * P],
                           w_gatex[:, n, :, :].rearrange("p g e -> p (g e)"), start=True, stop=True)
                        m = mm(ps[:, q + NE * NE:q + LG], den_t[:, t * P:(t + 1) * P], pick[:, :],
                               start=True, stop=True)
                else:
                    h = int(key[-1])
                    ps = job(b, n, key, False)
                    for t in range(4):
                        m = pe.transpose(ps[:, t * P:(t + 1) * P],
                                         o_t[:, h * HALF + t * P:h * HALF + (t + 1) * P], ident[:, :])
                m.then_inc(job_pe, 1)

            def warm(n):
                if n:
                    pe.wait_ge(exp_act, n * NT)
                for _ in range(WARM):
                    mm(ST[0][:, :], identb[:, :], mask_kq[:, :].unsqueeze(1).broadcast_to([P, 4, P]), start=True, stop=True)

            def attention(b, k):
                for key in PROJ:
                    project(b, 0, key)
                for t in range(NT):
                    if k >= LAG and t % TAIL_EVERY == TAIL_EVERY - 1:
                        tail(TAIL_PE[t // TAIL_EVERY])
                    for n, key in JOB_AT[-1].get(t, []):
                        project(b, n, key)
                    max_tile(b, 0, t, k)
                if k >= LAG:
                    pe.wait_ge(tail_dve, at(T_DVE, "om1"))
                max_rows(b, 0, False)
                for n in range(NH):
                    warm(n)
                    for t in range(NT):
                        for m, key in JOB_AT[n].get(t, []):
                            if m == n + 1:
                                project(b, m, key)
                            else:
                                gate(b, m, key)
                        if n == NH - 1 and k < B and t % NE == 0 and t // NE in POST_PE_AT:
                            post(b + 1, k, POST_PE_AT[t // NE])
                        score_tile(b, n, t, k)
                        for m in max_tiles(n, t):
                            max_tile(b, n + 1, m, k)
                        if t >= NE and t % NE == 1:
                            values(n, t // NE - 1)
                        elif t >= NE and t % NE == 3:
                            sums(n, t // NE - 1)
                    values(n, NG - 1)
                    sums(n, NG - 1)
                    if n + 1 < NH:
                        max_rows(b, n + 1, False)
                for key in GATE:
                    gate(b, NH - 1, key)

            def post(b, k, stage):
                if stage == "resid" and k >= LAG:
                    return
                if stage == "agg":
                    pe.wait_ge(neigh_dve, T)
                    if k >= 1:
                        pe.wait_ge(comb_dve, NH)
                elif stage == "xn":
                    pe.wait_ge(rows_in, 32 * (b + 1))
                elif stage == "xt":
                    pe.wait_ge(post_dve, at(POST_DVE, "xn2"))
                for h in range(2):
                    if stage in ("xn", "h"):
                        pe.wait_ge(post_act, at(POST_ACT, f"{'agg' if stage == 'xn' else 'xn'}{h}"))
                    if stage == "resid":
                        pe.wait_ge(post_act, at(POST_ACT, f"xt{h}"))
                    for t in range(4):
                        i = 4 * h + t
                        c = slice(i * P, (i + 1) * P)
                        ps = MX[h][:, t * P:(t + 1) * P]
                        if stage == "h":
                            mm(ps, xn_t[:, c], w_gnn[:, 0, :], start=True, stop=False)
                            mm(ps, agg_t[:, c], w_gnn[:, 1, :], start=False, stop=False)
                            m = mm(ps, ones_row[:, :], b_gnn[:, :], start=False, stop=True)
                        elif stage == "resid":
                            mm(ps, xn2_t[:, c], w_hl[:, :], start=True, stop=False)
                            m = mm(ps, ones_row[:, :], b_hlrow[:, :], start=False, stop=True)
                        else:
                            src = {"agg": agg, "xn": xnr, "xt": xn2}[stage]
                            m = pe.transpose(ps, src[:, i, :], ident[:, :])
                    m.then_inc(resid_pe if stage == "resid" else post_pe, 1)

            def tail(stage):
                c2 = lambda h: slice(int(h) * HALF, (int(h) + 1) * HALF)
                src, w, s, names, key = {
                    "t": (ty, None, tail_dve, T_DVE, "y"),
                    "m1": (ty_t, head_avg, tail_act, T_ACT, "t"),
                    "v1": (tsq, head_avg, tail_act, T_ACT, "sq"),
                    "h1": (tfx, w_fc1, tail_act, T_ACT, "fx"),
                    "h2": (tz, w_fc2, tail_dve, T_DVE, "h1"),
                    "m2": (tz, head_avg, tail_dve, T_DVE, "z"),
                    "v2": (tsq, head_avg, tail_act, T_ACT, "sz"),
                    "lg": (tfo, w_fg, tail_act, T_ACT, "fo"),
                    "rw": (tfo, None, tail_dve, T_DVE, "ls"),
                }[stage]
                for h in "01":
                    pe.wait_ge(s, at(names, key + h))
                    ps = ST[int(h)]
                    for t in range(4):
                        col = (4 * int(h) + t) * P
                        if w is None:
                            m = pe.transpose(ps[:, t * P:(t + 1) * P], src[:, col:col + P], ident[:, :])
                        elif stage == "lg":
                            m = mm(ps[:, t * NH:(t + 1) * NH], src[:, col:col + P], w[:, :],
                                   start=True, stop=True)
                        elif t == 0:
                            m = mm(ps[:, :], w[:, :], src[:, c2(h)], start=True, stop=True)
                    m.then_inc(tail_pe, 1)

            def phase(p, kind=None):
                k = p if kind is None else kind
                if 1 <= k <= B:
                    attention(p - 1, k)
                elif k == 0:
                    for stage in POST_PE_AT.values():
                        post(p, k, stage)
                elif k > B:
                    for stage in TAIL_PE:
                        tail(stage)

            phases(pe, phase, BARRIER[0])

        @block.vector
        def _(dve):
            dve.wait_ge(s_wload, 16 * (2 + 12 + 8))
            dve.wait_ge(s_const, 3)
            dve.wait_ge(s_wload2, 16 * (5 + 4 * 7))
            dve.tensor_copy(prio[:, :], prio_i)
            for e in range(NE):
                q = slice(D * e, D * e + D)
                dve.tensor_copy(w_gatex[q, :, :, e], w_gate[q, :, :])
            for r in range(4):
                dve.tensor_copy(w_hlrep[:, :, r, :], w_hl[:, :].rearrange("p (n d) -> p n d", d=D))
            for i in range(2):
                dve.memset(k_st[i][96:128, :].bitcast(F32), 0.0).then_inc(s_wready, 1)
                dve.wait_ge(s_wready, i + 1)
                dve.memset(k_st[i][96:97, :].bitcast(F32), 1.0)
            dve.tensor_copy(w_hi[:, :, :], w_in[:, :, :]).then_inc(s_wready, 1)
            dve.wait_ge(s_wready, 3)
            dve.tensor_tensor(w_lo[:, :, :], w_in[:, :, :], w_hi[:, :, :].bitcast(F32), ALU.subtract)\
               .then_inc(s_wready, 1)
            dve.wait_ge(s_wready, 4)
            for r in range(4):
                q = slice(D * r, D * r + D)
                src = (w_hi if r % 2 == 0 else w_lo)
                for c in range(3):
                    dve.tensor_copy(w_q[q, :, c, :], src[q, 0:16, :].bitcast(F32))
                    dve.tensor_copy(w_k[q, :, c, :], src[q, 16:20, :].bitcast(F32))
                last = dve.tensor_copy(w_v[q, :, :], src[q, 20:24, :].bitcast(F32))
            last.then_inc(s_wready, 1)

            def moments(src, st, m, s, base):
                for t in range(T):
                    last = dve.bn_stats(st[:, t, :], src[:, t, :])
                last.then_inc(s, 1)
                dve.wait_ge(s, base + 1)
                for t in range(T):
                    last = dve.bn_aggr(m[:, t, :], st[:, t, :])
                last.then_inc(s, 1)

            def normalise(src, m, rs, dst, s, base, std_act, std_value):
                dve.wait_ge(std_act, std_value)
                dve.reciprocal(rs[:, :], rs[:, :]).then_inc(s, 1)
                dve.wait_ge(s, base + 3)
                for t in range(T):
                    last = dve.tensor_scalar(dst[:, t, :], src[:, t, :], m[:, t, 0:1], rs[:, t:t + 1],
                                             ALU.subtract, ALU.mult)
                last.then_inc(s, 1)

            def pre(b, k):
                dve.wait_ge(x_in, 16 * (b + 1))
                if k >= 0:
                    dve.wait_ge(table_stored, 16 * b)
                moments(xa, stats, mv, pre_step, 0)
                normalise(xa, mv, rstd, xn, pre_step, 0, pre_act, 1)
                if k >= 0:
                    dve.tensor_scalar(prio[:, :], prio[:, :], float(-N), None, ALU.add)\
                       .then_inc(pre_step, 1)

            def rank(b, i, step):
                if step == 0:
                    dve.wait_ge(adj_in[i % 2], (b * (T // 2) + i // 2 + 1) * 16)
                    if i > 0:
                        dve.wait_ge(rank_step, rank_at(i, 0))
                    elif not (isinstance(b, int) and b == 0):
                        dve.wait_ge(pre_step, NORMED + 1)
                    dve.scalar_tensor_tensor(score[:, :], adj_t[i % 2][:, :], 0.0, prio[:, :],
                                             ALU.not_equal, ALU.mult).then_inc(rank_step, 1)
                    return
                dve.wait_ge(rank_step, rank_at(i, step))
                r, what = divmod(step - 1, 2)
                eight = top[:, i, 8 * r:8 * r + 8] if r < ROUNDS else None
                if step == INDEXED:
                    dve.tensor_scalar(index[:, i, :], top[:, i, :], -1.0, float(ZROW),
                                      ALU.mult, ALU.add).then_inc(index_ready, 1)
                elif step == FLOORED:
                    dve.tensor_scalar(floor[:, i:i + 1], top[:, i, TOP:TOP + 1], 0.0, NEG,
                                      ALU.is_gt, ALU.mult).then_inc(rank_step, 1)
                elif what == 0:
                    dve.max(eight, score[:, :]).then_inc(rank_step, 1)
                else:
                    dve.match_replace(score[:, :], eight, score[:, :], 0.0).then_inc(rank_step, 1)

            def neighbours(b, i, step):
                if step == 0:
                    dve.wait_ge(gather_in[i % 2], (b * (T // 2) + i // 2 + 1) * 16 * TOP)
                    dve.tensor_reduce(agg[:, i, :], fetched[i % 2][:, :, :].rearrange("p r c -> p c r"),
                                      AX.X, ALU.max).then_inc(fetched_read, 1)
                else:
                    dve.wait_ge(fetched_read, b * T + i + 1)
                    dve.tensor_scalar(agg[:, i, :], agg[:, i, :], floor[:, i:i + 1], None, ALU.max)\
                       .then_inc(neigh_dve, 1)

            def gnn_step(p, k, item):
                what, i, r = item
                if what == "max" and 0 <= k < B:
                    neighbours(p, i, r)
                elif what == "rank" and k < B - 1:
                    rank(p + 1, i, r)

            def post(b, k, stage):
                base = at(POST_DVE, "x21")
                if stage == "x2":
                    for h in range(2):
                        dve.wait_ge(post_pe, at(POST_PE, f"h{h}"))
                        if h == 0:
                            dve.wait_ge(rows_in, 32 * (b + 1))
                            if k >= 1:
                                dve.wait_ge(x2_stored, 16 * b)
                        ts = slice(4 * h, 4 * h + 4)
                        dve.scalar_tensor_tensor(x2[:, ts, :],
                                                 MX[h][:, :].rearrange("p (t c) -> p t c", c=C), 0.0,
                                                 xr[:, ts, :], ALU.max, ALU.add).then_inc(post_dve, 1)
                    dve.wait_ge(post_dve, base)
                    moments(x2, stats2, mv2, post_dve, base)
                elif stage == "xn2":
                    normalise(x2, mv2, rstd2, xn2, post_dve, base, post_act, at(POST_ACT, "std"))
                elif k < LAG:
                    for h in range(2):
                        dve.wait_ge(resid_pe, h + 1)
                        ts = slice(4 * h, 4 * h + 4)
                        src = MX[h][:, :].rearrange("p (t c) -> p t c", c=C)
                        if isinstance(b, int):
                            c = slice(b * D, (b + 1) * D)
                        else:
                            c = bass.ds(b * D, D)
                        dve.tensor_copy(resid[:, ts, c], src[:, :, c]).then_inc(resid_dve, 1)

            def project(n, key):
                if key == "v":
                    return
                c = slice(int(key[-1]) * HALF, (int(key[-1]) + 1) * HALF)
                dve.wait_ge(proj_act, pact_at(n, key))
                q, full, dst = {
                    "s": (slice(64, 128), sx_rep[n % 2][:, c], sx_st[:, c]),
                    "k": (slice(32, 64), job_bank(n, key)[:, :], k_st[n % 2][:, c]),
                    "q": (slice(64, 96), job_bank(n, key)[:, :],
                          q_st[n % 2][:, int(key[1]) if key[0] == "q" else 0, c]),
                }[key[0]]
                dve.tensor_tensor(dst[q], full[q], dst[q].bitcast(F32), ALU.subtract)\
                   .then_inc(proj_dve, 1)

            def max_tile(b, n, t):
                e, m = divmod(t, len(MAXT))
                i, kb, w = MAXT[m]
                dve.wait_ge(mx_pe, n * NT + t + 1)
                dst = mx[:, e, i:i + 1] if kb == 0 else mxb[:, e, i - 4:i - 3]
                dve.tensor_reduce(dst, MX[t % 2][:, 0:w], AX.X, ALU.max).then_inc(mx_dve, 1)

            def combine(b, n):
                dve.wait_ge(mx_dve, (n + 1) * NT)
                dve.tensor_tensor(mx[:, :, 4:8], mx[:, :, 4:8], mxb[:, :, :], ALU.max)\
                   .then_inc(comb_dve, 1)

            def outputs(b, n, h):
                c = slice(h * HALF, (h + 1) * HALF)
                dve.wait_ge(pv_pe, n * NG + LASTG[h] + 1)
                dve.scalar_tensor_tensor(o_t[:, c], sx_rep[n % 2][:, c], 0.0, PVO[:, :],
                                         ALU.not_equal, ALU.mult).then_inc(out_dve, 1)

            def over(small, like):
                return small.unsqueeze(len(small.shape)).broadcast_to(like)

            def softmax4(src, work, part, exped, dst, s, a_sem, a_value, at_step, keys):
                t = src.shape[1]
                dve.tensor_reduce(part[0], src, AX.X, ALU.max).then_inc(s, 1)
                dve.wait_ge(s, at_step(keys[0]))
                dve.tensor_tensor(work, src, over(part[0], [P, t, 4]), ALU.subtract).then_inc(s, 1)
                dve.wait_ge(a_sem, a_value)
                dve.tensor_reduce(part[1], exped, AX.X, ALU.add).then_inc(s, 1)
                dve.wait_ge(s, at_step(keys[2]))
                dve.reciprocal(part[2], part[1]).then_inc(s, 1)
                dve.wait_ge(s, at_step(keys[3]))
                dve.tensor_tensor(dst, exped, over(part[2], [P, t, 4]), ALU.mult).then_inc(s, 1)
                dve.wait_ge(s, at_step(keys[4]))

            def gate(b, n, k):
                step = lambda key: gate_at(n, key)
                dve.wait_ge(job_pe, job_at(n, "lg"))
                lgs = job_bank(n, "lg")[:, 0:T * LG].rearrange("p (t c) -> p t c", c=LG)
                dve.reciprocal(rden[:, :, :], lgs[:, :, NE * NE:LG]).then_inc(gate_dve, 1)
                dve.wait_ge(gate_dve, step("rd"))
                dve.tensor_tensor(part_lg[:, :, :, :],
                                  lgs[:, :, 0:NE * NE].rearrange("p t (g e) -> p t g e", e=NE),
                                  rden[:, :, :].unsqueeze(2).broadcast_to([P, T, NE, NE]), ALU.mult)\
                   .then_inc(gate_dve, 1)
                dve.wait_ge(gate_dve, step("pl"))
                dve.tensor_reduce(lg[:, :, :], part_lg[:, :, :, :], AX.X, ALU.add).then_inc(gate_dve, 1)
                dve.wait_ge(gate_dve, step("sl"))
                dve.tensor_tensor(lg[:, :, :], lg[:, :, :],
                                  b_gate[:, n:n + 1, :].broadcast_to([P, T, NE]), ALU.add)\
                   .then_inc(gate_dve, 1)
                dve.wait_ge(gate_dve, step("lg"))
                softmax4(lg[:, :, :], lg_s[:, :, :], [g8[:, j, :] for j in range(3)], lg_e[:, :, :],
                         gs[:, :, :], gate_dve, gate_act, n + 1, step,
                         ["max", "sub", "sum", "rec", "gs"])
                dve.tensor_tensor(gs[:, :, :], gs[:, :, :], rden[:, :, :], ALU.mult).then_inc(gate_dve, 1)
                dve.wait_ge(gate_dve, step("gr"))
                if n == 0 and k != 1:
                    dve.wait_ge(mix_stored, 16 * b)
                for h in range(2):
                    dve.wait_ge(job_pe, job_at(n, f"row{h}"))
                    ts = slice(4 * h, 4 * h + 4)
                    c = slice(h * HALF, (h + 1) * HALF)
                    dve.tensor_tensor(wmix[:, c].rearrange("p (t d) -> p t d", d=D),
                                      job_bank(n, f"row{h}")[:, :].rearrange("p (t d) -> p t d", d=D),
                                      over(gs[:, ts, :].rearrange("p t e -> p (t e)"), [P, 16, D]),
                                      ALU.mult).then_inc(gate_dve, 1)
                    dve.wait_ge(gate_dve, step(f"w{h}"))
                    dve.tensor_reduce(mixed[:, ts, n, :], wmix[:, c]
                                      .rearrange("p (t e d) -> p t d e", e=NE, d=D),
                                      AX.X, ALU.add).then_inc(gate_dve, 1)

            def attention(p, k):
                b = p - 1
                for key in PROJ:
                    project(0, key)
                if k < B - 1:
                    pre(p + 1, k)
                for t in range(NT):
                    if k >= LAG and t % TAIL_EVERY == 0:
                        tail(p - LAG, TAIL_DVE[t // TAIL_EVERY])
                    for n, key in JOB_AT[-1].get(t, []):
                        project(n, key)
                    max_tile(b, 0, t)
                    for item in gnn_steps(-1, t):
                        gnn_step(p, k, item)
                combine(b, 0)
                for n in range(NH):
                    for t in range(NT):
                        for m, key in JOB_AT[n].get(t, []):
                            if m == n + 1:
                                project(m, key)
                            elif key == "row1":
                                gate(b, m, k)
                        for m in max_tiles(n, t):
                            max_tile(b, n + 1, m)
                        for item in gnn_steps(n, t):
                            gnn_step(p, k, item)
                        if t == NE * (LASTG[0] + 2):
                            outputs(b, n, 0)
                        if n == NH - 1 and k < B and t % NE == 0 and t // NE in POST_DVE_AT:
                            post(p, k, POST_DVE_AT[t // NE])
                    if n + 1 < NH:
                        combine(b, n + 1)
                    outputs(b, n, 1)
                gate(b, NH - 1, k)

            def tail(b, stage):
                c2 = lambda h: slice(int(h) * HALF, (int(h) + 1) * HALF)
                r3 = lambda t_, h: t_[:, c2(h)].rearrange("p (t c) -> p t c", c=C)
                psl = lambda h: ST[h][:, 0:4 * NH].rearrange("p (t n) -> p t n", n=NH)
                r4 = lambda a: a.rearrange("p (g d) -> p g d", d=D)
                hs = [slice(0, 4), slice(4, 8)]

                def did(i):
                    i.then_inc(tail_dve, 1)

                def mine(key):
                    dve.wait_ge(tail_dve, at(T_DVE, key))

                if stage == "y":
                    dve.wait_ge(tail_in, 32 * (b + 1))
                    for h in range(2):
                        did(dve.tensor_tensor(r3(ty, h), tm[:, hs[h], :], resid[:, hs[h], :], ALU.add))
                elif stage in ("yc", "zc"):
                    for h in "01":
                        dve.wait_ge(tail_pe, at(T_PE, ("m1" if stage == "yc" else "m2") + h))
                        did(dve.tensor_tensor(tyc[:, c2(h)], (ty_t if stage == "yc" else tz)[:, c2(h)],
                                              ST[int(h)][:, :], ALU.subtract))
                elif stage in ("yn", "zn"):
                    for h in "01":
                        dve.wait_ge(tail_act, at(T_ACT, ("s1" if stage == "yn" else "s2") + h))
                        did(dve.tensor_tensor(ty[:, c2(h)], tyc[:, c2(h)], trs[:, c2(h)], ALU.mult))
                elif stage in ("h1", "h2"):
                    for h in "01":
                        dve.wait_ge(tail_act, at(T_ACT, ("r1" if stage == "h1" else "r2") + h))
                        did(dve.scalar_tensor_tensor(tz[:, c2(h)], tfx[:, c2(h)], 0.0, tr[:, c2(h)],
                                                     ALU.not_equal, ALU.mult))
                    if stage == "h2":
                        for h in "01":
                            mine("h2" + h)
                            did(dve.tensor_tensor(tz[:, c2(h)], tz[:, c2(h)], tfx[:, c2(h)], ALU.add))
                elif stage == "soft":
                    for h in range(2):
                        dve.wait_ge(tail_pe, at(T_PE, f"lg{h}"))
                        did(dve.tensor_reduce(t8[:, 0, hs[h]], psl(h), AX.X, ALU.max))
                    for h in range(2):
                        mine(f"lm{h}")
                        did(dve.tensor_tensor(tl[:, 0, hs[h], :], psl(h),
                                              over(t8[:, 0, hs[h]], [P, 4, NH]), ALU.subtract))
                elif stage == "out":
                    for h in range(2):
                        dve.wait_ge(tail_act, at(T_ACT, f"ex{h}"))
                        did(dve.tensor_reduce(t8[:, 1, hs[h]], tl[:, 1, hs[h], :], AX.X, ALU.add))
                    for h in range(2):
                        mine(f"su{h}")
                        did(dve.reciprocal(t8[:, 2, hs[h]], t8[:, 1, hs[h]]))
                    for h in range(2):
                        mine(f"re{h}")
                        did(dve.tensor_tensor(tl[:, 2, hs[h], :], tl[:, 1, hs[h], :],
                                              over(t8[:, 2, hs[h]], [P, 4, NH]), ALU.mult))
                    for h in range(2):
                        dve.wait_ge(tail_pe, at(T_PE, f"rw{h}"))
                        mine(f"gs{h}")
                        did(dve.tensor_tensor(r4(ty[:, c2(h)]), r4(ST[h][:, :]),
                                              over(tl[:, 2, hs[h], :].rearrange("p t n -> p (t n)"),
                                                   [P, 16, D]), ALU.mult))
                    for h in range(2):
                        mine(f"om{h}")
                        did(dve.tensor_tensor(tout[:, hs[h], :], r3(ty, h), tx[:, hs[h], :], ALU.add))

            def phase(p, kind=None):
                k = p if kind is None else kind
                if 1 <= k <= B:
                    attention(p, k)
                    return
                if k < 1:
                    pre(p + 1, k)
                    for w in GNN:
                        for item in GNN[w]:
                            gnn_step(p, k, item)
                if k == 0:
                    for stage in POST_DVE_AT.values():
                        post(p, k, stage)
                if k > B:
                    for stage in TAIL_DVE:
                        tail(p - LAG, stage)

            phases(dve, phase, BARRIER)


def kernel(x, adj, L0_gnn_W, L0_gnn_b, L0_ffn_hl_w, L0_ffn_hl_b, L0_ffn_wq, L0_ffn_wk, L0_ffn_wv,
           L0_ffn_gate_w, L0_ffn_gate_b, L0_ffn_ln_g, L0_ffn_ln_b, L0_ffn_fc1_w, L0_ffn_fc1_b,
           L0_ffn_fc2_w, L0_ffn_fc2_b, L0_ffn_fnorm_g, L0_ffn_fnorm_b, L0_ffn_fgate_w):
    import numpy as np
    import concourse.bacc as bacc
    from concourse.bass_utils import run_bass_kernel_spmd

    a = lambda v, *shape: np.ascontiguousarray(np.asarray(v).reshape(shape))
    t = lambda v, *axes: np.ascontiguousarray(np.asarray(v).transpose(axes))
    nh, d, h = np.asarray(L0_ffn_hl_w).shape
    ne = np.asarray(L0_ffn_wq).shape[1]
    ins = {
        "x": np.asarray(x), "adj": np.asarray(adj), "gnn_w": np.asarray(L0_gnn_W),
        "gnn_b": a(L0_gnn_b, 1, h),
        "hl_t": t(L0_ffn_hl_w, 2, 0, 1).reshape(h, nh * d),
        "hl_brow": a(L0_ffn_hl_b, 1, nh * d), "hl_bcol": t(L0_ffn_hl_b, 1, 0),
        "wq_t": t(L0_ffn_wq, 3, 0, 1, 2).reshape(d, nh * ne, d),
        "wk_t": t(L0_ffn_wk, 2, 0, 1), "wv_t": t(L0_ffn_wv, 2, 0, 1),
        "gate_t": t(L0_ffn_gate_w, 2, 0, 1), "gate_b": np.asarray(L0_ffn_gate_b),
        "ln_g": a(L0_ffn_ln_g, d, 1), "ln_b": a(L0_ffn_ln_b, d, 1),
        "fc1_t": t(L0_ffn_fc1_w, 1, 0), "fc1_b": a(L0_ffn_fc1_b, d, 1),
        "fc2_t": t(L0_ffn_fc2_w, 1, 0), "fc2_b": a(L0_ffn_fc2_b, d, 1),
        "fn_g": a(L0_ffn_fnorm_g, d, 1), "fn_b": a(L0_ffn_fnorm_b, d, 1),
        "fgate_t": t(L0_ffn_fgate_w, 1, 0),
    }
    nc = bacc.Bacc("TRN2", target_bir_lowering=False, num_devices=1)
    args = [nc.dram_tensor(f"in_{k}", v.shape, mybir.dt.from_np(v.dtype), kind="ExternalInput").ap()
            for k, v in ins.items()]
    out = nc.dram_tensor("out", ins["x"].shape, mybir.dt.float32, kind="ExternalOutput").ap()
    build(nc, *args, out)
    r = run_bass_kernel_spmd(nc, [{f"in_{k}": v for k, v in ins.items()}], core_ids=[0])
    return r.results[0]["out"]
```

```python
import concourse.bass as bass
from concourse import mybir
from contextlib import ExitStack


def build(nc, x, adj, gnn_w, gnn_b, hl_t, hl_brow, hl_bcol, wq_t, wk_t, wv_t, gate_t, gate_b,
          ln_g, ln_b, fc1_t, fc1_b, fc2_t, fc2_b, fn_g, fn_b, fgate_t, out):
    F32, F32R, BF16 = mybir.dt.float32, mybir.dt.float32r, mybir.dt.bfloat16
    U32, I32 = mybir.dt.uint32, mybir.dt.int32
    ALU = mybir.AluOpType
    ACT = mybir.ActivationFunctionType
    AX = mybir.AxisListType

    B, N, C = x.shape
    P = 128
    T = N // P
    NH, NE, D = 4, 4, 32
    TOP = 25
    ROUNDS = -(-(TOP + 1) // 8)
    ZROW = B * N
    NEG = -1.0e30
    HALF = N // 2
    SCALE = float(D) ** 0.5
    EPS1, EPS2 = 1e-5, 1e-8
    WARM = 7
    LAG = 4

    rows = lambda a: a.rearrange("b (t p) c -> b p t c", p=P)
    x_v, out_v = rows(x), rows(out)
    adj_v = adj.rearrange("b (t p) m -> b t p m", p=P)
    table = nc.dram_tensor("table", (B * N + 8, C), F32, kind="Internal").ap()
    table_v = rows(table[0:B * N, :].rearrange("(b n) c -> b n c", n=N))
    x2_d = rows(nc.dram_tensor("x2_rows", (B, N, C), F32, kind="Internal").ap())
    mix_d = rows(nc.dram_tensor("mixed_rows", (B, N, C), F32, kind="Internal").ap())

    ctx = ExitStack()
    with ctx:
        sb = lambda name, shape, dt=F32: ctx.enter_context(nc.sbuf_tensor(name, shape, dt))
        sem = lambda name: ctx.enter_context(nc.semaphore(name))

        ident = sb("ident", [P, P])
        identb = sb("identb", [P, P], BF16)
        mask_qk = sb("mask_qk", [P, P], BF16)
        mask_kq = sb("mask_kq", [P, P], BF16)
        ones_row = sb("ones_row", [1, P])
        ones_den = sb("ones_den", [P, D])
        head_avg = sb("head_avg", [P, P])
        prio = sb("prio", [P, N])
        zrow = sb("zrow", [8, C])
        eps = sb("eps", [P, 2])
        ready = sb("ready", [1, 1])
        w_gnn = sb("w_gnn", [P, 2, C])
        b_gnn = sb("b_gnn", [1, C])
        w_hl = sb("w_hl", [P, NH * D])
        w_hlrep = sb("w_hlrep", [P, NH, 4, D])
        b_hlrow = sb("b_hlrow", [1, NH * D])
        b_hlrep = sb("b_hlrep", [P, NH])
        NW = NH * NE + NH + NH
        w_q = sb("w_q", [P, NH * NE, 4, D], F32R)
        w_k = sb("w_k", [P, NH, 3, D], F32R)
        w_v = sb("w_v", [P, NH, D], F32R)
        w_gate = sb("w_gate", [P, NH, NE])
        w_gatex = sb("w_gatex", [P, NH, NE, NE])
        pick = sb("pick", [P, NE])
        b_gate = sb("b_gate", [P, NH, NE])
        w_fc1 = sb("w_fc1", [P, P])
        w_fc2 = sb("w_fc2", [P, P])
        w_fg = sb("w_fg", [P, NH])
        cols = {k: sb(k + "_col", [P, 1]) for k in ("ln_g", "ln_b", "fc1_b", "fc2_b", "fn_g", "fn_b")}
        xa = sb("xa", [P, T, C])
        stats = sb("stats", [P, T, 6])
        mv = sb("mv", [P, T, 2])
        rstd = sb("rstd", [P, T])
        xn = sb("xn", [P, T, C])
        adj_t = [sb(f"adj_t{i}", [P, N], I32) for i in range(2)]
        score = sb("score", [P, N])
        prio_i = score[:, :].bitcast(I32)
        top = sb("top", [P, T, 8 * ROUNDS])
        index = sb("index", [P, T, 8 * ROUNDS], U32)
        floor = sb("floor", [P, T])
        fetched = [sb(f"fetched{i}", [P, TOP, C]) for i in range(2)]
        weights = lambda i, k: fetched[i][:, :, :].rearrange("p r c -> p (r c)")\
            [:, k * NW * D:(k + 1) * NW * D].rearrange("p (w d) -> p w d", d=D)
        w_in, w_hi, w_lo = weights(0, 0), weights(1, 0).bitcast(F32R), weights(1, 1).bitcast(F32R)
        agg = sb("agg", [P, T, C])
        xr = sb("xr", [P, T, C])
        xnr = sb("xnr", [P, T, C])
        agg_t = sb("agg_t", [P, N])
        xn_t = sb("xn_t", [P, N])
        x2 = sb("x2", [P, T, C])
        stats2 = sb("stats2", [P, T, 6])
        mv2 = sb("mv2", [P, T, 2])
        rstd2 = sb("rstd2", [P, T])
        xn2 = sb("xn2", [P, T, C])
        xn2_t = sb("xn2_t", [P, N])
        resid = sb("resid", [P, T, NH * D])
        sx_rep = [sb(f"sx_rep{i}", [P, N]) for i in range(2)]
        sx_st = sb("sx_st", [P, N], F32R)
        q_st = [sb(f"q_st{i}", [P, NE, N], F32R) for i in range(2)]
        k_st = [sb(f"k_st{i}", [P, N], F32R) for i in range(2)]
        v_sb = [sb(f"v_sb{i}", [P, T, D]) for i in range(2)]
        mx = sb("mx", [P, NE, T])
        mxb = sb("mxb", [P, NE, T // 2])
        mrow = sb("mrow", [NE * T, P], F32R)
        NP = 8
        probs_all = sb("probs", [P, NP * 512])
        probs = [probs_all[:, 512 * i:512 * (i + 1)] for i in range(NP)]
        o_t = sb("o_t", [P, N])
        den_t = sb("den_t", [P, N])
        lg = sb("lg", [P, T, NE])
        part_lg = sb("part_lg", [P, T, NE, NE])
        rden = sb("rden", [P, T, NE])
        lg_s = sb("lg_s", [P, T, NE])
        lg_e = sb("lg_e", [P, T, NE])
        gs = sb("gs", [P, T, NE])
        g8 = sb("g8", [P, 3, T])
        wmix = sb("wmix", [P, N])
        mixed = sb("mixed", [P, T, NH, D])
        tm = sb("tm", [P, T, C])
        tx = sb("tx", [P, T, C])
        ty_t, tyc, tsq, trs = (probs_all[:, N * i:N * (i + 1)] for i in range(4))
        ty = xn2[:, :, :].rearrange("p t c -> p (t c)")
        tfx, tr, tz, tfo = o_t[:, :], agg_t[:, :], wmix[:, :], xn_t[:, :]
        tl, tl2 = sb("tl", [P, 3, T, NH]), sb("tl2", [P, 3, T, NH])
        t8, t82 = sb("t8", [P, 3, T]), sb("t82", [P, 3, T])

        bank = [ctx.enter_context(nc.psum_tensor(f"bank{i}", [P, 512], F32)) for i in range(8)]
        part = lambda i, k: fetched[i][:, :, :].rearrange("p r c -> p (r c)")[:, k * N:(k + 1) * N]
        flat = lambda a: a[:, :, :].rearrange("p t c -> p (t c)")
        tile2 = lambda a: a[:, :].bitcast(F32).rearrange("p (t c) -> p t c", c=C)
        G, MX, ST, PVO, PVD = bank[0:2], bank[2:4], bank[4:6], bank[6], bank[7]

        s_wload = sem("s_wload")
        s_wload2 = sem("s_wload2")
        s_const = sem("s_const")
        s_masks = sem("s_masks")
        s_wready = sem("s_wready")
        s_zero = sem("s_zero")
        x_in = sem("x_in")
        adj_in = [sem(f"adj_in{i}") for i in range(2)]
        table_stored = sem("table_stored")
        index_ready = sem("index_ready")
        tile_begun = sem("tile_begun")
        gather_in = [sem(f"gather_in{i}") for i in range(2)]
        fetched_read = sem("fetched_read")
        rows_in = sem("rows_in")
        x2_stored, mix_stored = sem("x2_stored"), sem("mix_stored")
        tail_in, tail2_in = sem("tail_in"), sem("tail2_in")
        out_stored = sem("out_stored")
        mrow_in = sem("mrow_in")
        go_pe, go_act, go_sp = sem("go_pe"), sem("go_act"), sem("go_sp")

        in_phase = []

        def psem(name):
            in_phase.append(sem(name))
            return in_phase[-1]

        pre_step = psem("pre_step")
        pre_act = psem("pre_act")
        rank_step = psem("rank_step")
        neigh_dve = psem("neigh_dve")
        post_pe, post_act, post_dve = psem("post_pe"), psem("post_act"), psem("post_dve")
        resid_pe, resid_dve = psem("resid_pe"), psem("resid_dve")
        job_pe = psem("job_pe")
        proj_act, proj_dve = psem("proj_act"), psem("proj_dve")
        mx_pe, mx_dve = psem("mx_pe"), psem("mx_dve")
        comb_dve = psem("comb_dve")
        mrow_act = psem("mrow_act")
        st_pe, exp_act, pv_pe = psem("st_pe"), psem("exp_act"), psem("pv_pe")
        out_dve, den_act = psem("out_dve"), psem("den_act")
        gate_dve, gate_act = psem("gate_dve"), psem("gate_act")
        tail_pe, tail_act, tail_dve = psem("tail_pe"), psem("tail_act"), psem("tail_dve")

        tail2_pe, tail2_act, tail2_dve = psem("tail2_pe"), psem("tail2_act"), psem("tail2_dve")
        end_pe, end_act, end_sp = psem("end_pe"), psem("end_act"), psem("end_sp")
        BARRIER = [(end_pe, go_pe), (end_act, go_act), (end_sp, go_sp)]

        class Tail:
            def __init__(self, m, x, y, yt, yc, sq, rs, fx, r, z, fo, l, s8, bank, pe, act, dve, loaded):
                self.m, self.x, self.y, self.yt, self.yc, self.sq = m, x, y, yt, yc, sq
                self.rs, self.fx, self.r, self.z, self.fo, self.l, self.s8 = rs, fx, r, z, fo, l, s8
                self.bank, self.pe, self.act, self.dve, self.loaded = bank, pe, act, dve, loaded

        TAIL1 = Tail(m=tm, x=tx, y=ty, yt=ty_t, yc=tyc, sq=tsq, rs=trs, fx=tfx, r=tr, z=tz, fo=tfo,
                     l=tl, s8=t8, bank=ST, pe=tail_pe, act=tail_act, dve=tail_dve, loaded=tail_in)
        TAIL2 = Tail(m=tile2(adj_t[0]), x=tile2(adj_t[1]), y=flat(xn), yt=part(0, 0),
                     yc=part(0, 1), sq=part(0, 2), rs=part(1, 0), fx=part(1, 1), r=flat(xnr),
                     z=part(1, 2), fo=flat(xr), l=tl2, s8=t82, bank=MX,
                     pe=tail2_pe, act=tail2_act, dve=tail2_dve, loaded=tail2_in)

        RANK = 2 * ROUNDS + 2
        INDEXED, FLOORED = RANK - 2, RANK - 1
        rank_at = lambda i, step: i * (RANK - 1) + min(step, RANK - 2)
        NORMED = 4
        POST_PE = ["agg0", "agg1", "xn0", "xn1", "h0", "h1", "xt0", "xt1"]
        POST_ACT = ["agg0", "agg1", "xn0", "xn1", "std", "xt0", "xt1"]
        POST_DVE = ["x20", "x21", "stat", "aggr", "rstd", "xn2"]
        at = lambda names, k: names.index(k) + 1

        LG = NE * NE + NE

        PROJ = ["sx0", "sx1", "k0", "k1", "v"] + [f"q{e}{h}" for e in range(NE) for h in range(2)]
        GATE = ["lg", "row0", "row1"]
        JOBS = [(0, k) for k in PROJ] + [(1, k) for k in PROJ] + [(0, "m")]
        JOB_AT = {-1: {5 * (i // 2) + 1 + 2 * (i % 2): [(1, k)] for i, k in enumerate(PROJ)}}
        GATE_AT = {"lg": 2, "row0": 4, "row1": 5}
        MAX_FROM = {0: 2}
        for n in range(NH):
            JOB_AT[n] = {GATE_AT[k]: [(n - 1, k)] for k in GATE} if n else {}
            if 0 < n < NH - 1:
                JOB_AT[n][0] = [(n + 1, "sx0"), (n + 1, "sx1")]
                for i, k in enumerate(PROJ[2:]):
                    JOB_AT[n][6 + i] = [(n + 1, k)]
                MAX_FROM[n] = 6 + len(PROJ[2:])
            for slot in sorted(JOB_AT[n]):
                JOBS += JOB_AT[n][slot]
            if n + 1 < NH:
                JOBS += [(n + 1, "m")]
        JOBS += [(NH - 1, k) for k in GATE]
        assert len(set(JOBS)) == len(JOBS)
        JOB_BANK, BEFORE = {}, {}
        used = {}
        for n, k in JOBS:
            which = min(range(4 if k[0] in "kq" and n != 1 else 2),
                        key=lambda i: JOBS.index(used[i]) if i in used else i - 4)
            JOB_BANK[n, k], BEFORE[n, k] = (G + MX)[which], used.get(which)
            used[which] = (n, k)
        P_ACT = ["sxr0", "sx0", "sxr1", "sx1", "k0", "k1", "v"] + PROJ[5:]
        P_DVE = ["sx0", "sx1", "k0", "k1"] + PROJ[5:]
        GATE_STEPS = ["rd", "pl", "sl", "lg", "max", "sub", "sum", "rec", "gs", "gr",
                      "w0", "mix0", "w1", "mix1"]
        job_at = lambda n, k: JOBS.index((n, k)) + 1
        job_bank = lambda n, k: JOB_BANK[n, k]
        pact_at = lambda n, k: n * len(P_ACT) + P_ACT.index(k) + 1
        pdve_at = lambda n, k: n * len(P_DVE) + P_DVE.index(k) + 1
        gate_at = lambda n, k: n * len(GATE_STEPS) + GATE_STEPS.index(k) + 1

        def job_freed(n, k):
            if k in ("sx0", "sx1", "v"):
                return proj_act, pact_at(n, k)
            if k == "m":
                return mrow_act, n + 1
            if k in GATE:
                return gate_dve, gate_at(n, {"lg": "pl", "row0": "w0", "row1": "w1"}[k])
            return proj_dve, pdve_at(n, k)

        MAXT = [(i, kb, min(512, P * (i + 1) - 512 * kb)) for i in range(T) for kb in range(1 + i // 4)]
        STG = [(h, j, P * max(0, j - 4 * h)) for h in range(2) for j in range(4 * (h + 1))]
        NG, NT = len(STG), NE * len(STG)
        assert NT == NE * len(MAXT)
        max_tiles = lambda n, t: range(*(max(0, NT * (u - MAX_FROM[n]) // (NT - MAX_FROM[n]))
                                         for u in (t, t + 1))) if n in MAX_FROM else ()
        LASTG = [max(g for g in range(NG) if STG[g][0] == h) for h in range(2)]

        T_PE = [k + h for k in ("t", "m1", "v1", "h1", "h2", "m2", "v2", "lg", "rw") for h in "01"]
        T_ACT = [k + h for k in ("t", "sq", "l1", "s1", "fx", "r1", "r2", "sz", "l2", "s2", "fo", "ex")
                 for h in "01"]
        T_DVE = [k + h for k in ("y", "yc", "yn", "h1", "h2", "z", "zc", "zn",
                                 "lm", "ls", "su", "re", "gs", "om", "out") for h in "01"]

        TAIL_PE = ["t", "m1", "v1", "h1", "h2", "m2", "v2", "lg", "rw"]
        TAIL_DVE = ["y", None, "yc", "yn", "h1", "h2", "zc", "zn", "soft", "out"]
        TAIL_EVERY = 5
        assert TAIL_EVERY * (len(TAIL_DVE) - 1) < NT
        POST_PE_AT = {1: "agg", 3: "xn", 5: "h", 8: "xt", 10: "resid"}
        POST_ACT_AT = {2: "agg", 4: "xn", 7: "std", 9: "xt"}
        POST_DVE_AT = {6: "x2", 8: "xn2", 11: "resid"}
        TAIL_ACT_AT = {4: ["t"], 10: ["sq"], 14: ["l1", "s1"], 15: ["fx"], 19: ["r1"], 24: ["r2"],
                       30: ["sz"], 34: ["l2", "s2"], 35: ["fo"], 40: ["ex"]}

        tile_max = lambda i: [("max", i, s) for s in range(2)]
        tile_rank = lambda i: [("rank", i, s) for s in range(RANK)]
        GNN = {-1: tile_max(0) + tile_max(1) + tile_rank(0),
               0: tile_max(2) + tile_rank(1) + tile_max(3) + tile_rank(2),
               1: tile_max(4) + tile_rank(3) + tile_max(5),
               2: tile_max(6) + tile_rank(4) + tile_max(7),
               3: tile_rank(5) + tile_rank(6) + tile_rank(7)}
        SPAN = {-1: 40, 0: NT, 1: 40, 2: 40, 3: NT}
        gnn_steps = lambda w, t: GNN[w][len(GNN[w]) * t // SPAN[w]:len(GNN[w]) * (t + 1) // SPAN[w]]
        ADJ_LOADS = [(2,), (3, 4), (5,), (6,), (7,)]

        def phases(e, stages, mine):

            def phase(p, kind=None):
                stages(p, kind)
                if mine is BARRIER:
                    e.drain()
                    for end, _ in BARRIER:
                        e.wait_ge(end, 1)
                    e.sem_clear(range(in_phase[0].num, in_phase[-1].num + 1))
                    for _, go in BARRIER:
                        e.drain().then_inc(go, 1)
                elif mine is not None:
                    end, go = mine
                    e.drain().then_inc(end, 1)
                    e.wait_ge(go, 1)
                    e.sem_clear(go)

            phase(-1)
            phase(0)
            phase(1)
            with e.Fori(2, LAG) as p:
                phase(p, kind=2)
            with e.Fori(LAG, B - 1) as p:
                phase(p, kind=LAG)
            phase(B - 1)
            phase(B)
            phase(B + 1)

        block = ctx.enter_context(nc.Block())

        def wait(e, s, value):
            if not isinstance(value, int) or value > 0:
                e.wait_ge(s, value)

        @block.sync
        def _(sp):
            sp.dma_start(w_gnn[:, :, :], gnn_w.rearrange("(a p) o -> p a o", p=P)).then_inc(s_wload, 16)
            sp.dma_start(w_hl[:, :], hl_t).then_inc(s_wload, 16)
            for r in range(4):
                q = slice(D * r, D * r + D)
                sp.dma_start(w_in[q, 0:16, :], wq_t).then_inc(s_wload, 16)
                sp.dma_start(w_in[q, 16:20, :], wk_t).then_inc(s_wload, 16)
                sp.dma_start(w_in[q, 20:24, :], wv_t).then_inc(s_wload, 16)
            sp.wait_ge(s_const, 1)
            sp.dma_start(table[ZROW:ZROW + 8, :], zrow[:, :]).then_inc(s_zero, 16)
            for b in range(1, B):
                sp.dma_start(table_v[b], x2[:, :, :]).then_inc(s_zero, 16)
            for r in range(4):
                q = slice(D * r, D * r + D)
                sp.dma_start(w_fc1[q, q], fc1_t).then_inc(s_wload, 16)
                sp.dma_start(w_fc2[q, q], fc2_t).then_inc(s_wload, 16)

            def load_adj(b, i):
                if i >= 2:
                    sp.wait_ge(rank_step, rank_at(i - 2, 1))
                sp.dma_start(adj_t[i % 2][:, :], adj_v[b, i]).then_inc(adj_in[i % 2], 16)

            def phase(p, kind=None):
                k = p if kind is None else kind
                pre, post, att, tail = k < B - 1, 0 <= k < B, 1 <= k <= B, k >= LAG
                if pre:
                    sp.dma_start(xa[:, :, :], x_v[p + 1]).then_inc(x_in, 16)
                    for i in range(2):
                        load_adj(p + 1, i)
                if post:
                    sp.dma_start(xr[:, :, :], x_v[p]).then_inc(rows_in, 16)
                    wait(sp, table_stored, 16 * (p + 1))
                    sp.dma_start(xnr[:, :, :], table_v[p]).then_inc(rows_in, 16)
                def load_tail(u, b):
                    sp.dma_start(u.m[:, :, :], mix_d[b]).then_inc(u.loaded, 16)
                    sp.dma_start(u.x[:, :, :], x2_d[b]).then_inc(u.loaded, 16)

                def store_tail(u, b):
                    sp.wait_ge(u.dve, at(T_DVE, "out1"))
                    sp.dma_start(out_v[b], u.m[:, :, :]).then_inc(out_stored, 16)

                if tail:
                    if not pre:
                        sp.wait_ge(out_stored, 16 * (k - LAG + (k > B)))
                    sp.wait_ge(mix_stored, 16 * (B - 1 if k > B else p - LAG + 1))
                    load_tail(TAIL1, B - 2 if k > B else p - LAG)
                    if k > B:
                        sp.wait_ge(x2_stored, 16 * B)
                    if k >= B:
                        sp.wait_ge(mix_stored, 16 * (B if k > B else B - 2))
                        load_tail(TAIL2, B - 1 if k > B else B - LAG + 1)
                    store_tail(TAIL1, B - 2 if k > B else p - LAG)
                if pre:
                    if k == 0:
                        sp.wait_ge(s_zero, 16 * B)
                    wait(sp, pre_step, NORMED)
                    sp.dma_start(table_v[p + 1], xn[:, :, :]).then_inc(table_stored, 16)
                for n in range(NH + 1):
                    if pre:
                        for i in ADJ_LOADS[n]:
                            load_adj(p + 1, i)
                    if n < NH and att:
                        wait(sp, mrow_act, n + 1)
                        sp.dma_start(q_st[n % 2][96:97, :, :].bitcast(F32)
                                     .rearrange("a e (t c) -> a (e t) c", c=P),
                                     mrow[:, :].bitcast(F32)).then_inc(mrow_in, 16)
                if tail and pre:
                    wait(sp, out_stored, 16 * (p - LAG + 1))
                if att:
                    wait(sp, gate_dve, gate_at(NH - 1, "mix1"))
                    sp.dma_start(mix_d[p - 1], mixed[:, :, :, :].rearrange("p t n d -> p t (n d)"))\
                      .then_inc(mix_stored, 16)
                if k >= B:
                    store_tail(TAIL2, B - 1 if k > B else B - LAG + 1)
                if post:
                    wait(sp, post_dve, at(POST_DVE, "x21"))
                    sp.dma_start(x2_d[p], x2[:, :, :]).then_inc(x2_stored, 16)

            phases(sp, phase, BARRIER[2])
            sp.wait_ge(out_stored, 16 * B)

        @block.gpsimd
        def _(pool):
            pool.memset(zrow[:, :], 0.0)
            pool.memset(x2[:, :, :], 0.0)
            pool.memset(w_fc1[:, :], 0.0)
            pool.memset(w_fc2[:, :], 0.0).then_inc(s_const, 1)
            pool.memset(ident[:, :], 0.0)
            pool.memset(identb[:, :], 0.0)
            pool.memset(mask_qk[:, :], 0.0)
            pool.memset(mask_kq[:, :], 0.0)
            pool.memset(ones_row[:, :], 1.0)
            pool.memset(eps[:, 0:1], EPS1)
            pool.memset(eps[:, 1:2], EPS2)
            pool.memset(ones_den[:, :], 1.0)
            pool.memset(pick[:, :], 0.0)
            pool.memset(w_gatex[:, :, :, :], 0.0)
            pool.memset(head_avg[:, :], 0.0).then_inc(s_const, 1)
            pool.wait_ge(s_const, 2)
            for m in (ident, identb):
                pool.affine_select(out=m[:, :], in_=m[:, :], compare_op=ALU.not_equal, fill=1.0,
                                   base=0, pattern=[[-1, P]], channel_multiplier=1).then_inc(s_masks, 1)
            pool.affine_select(out=pick[:, :], in_=pick[:, :], compare_op=ALU.not_equal, fill=1.0,
                               base=0, pattern=[[-D, NE]], channel_multiplier=1).then_inc(s_masks, 1)
            pool.affine_select(out=mask_qk[:, :], in_=mask_qk[:, :], compare_op=ALU.is_ge, fill=NEG,
                               base=0, pattern=[[-1, P]], channel_multiplier=1).then_inc(s_masks, 1)
            pool.affine_select(out=mask_kq[:, :], in_=mask_kq[:, :], compare_op=ALU.is_ge, fill=NEG,
                               base=0, pattern=[[1, P]], channel_multiplier=-1).then_inc(s_masks, 1)
            pool.wait_ge(s_masks, 5)
            for r in range(4):
                q = slice(D * r, D * r + D)
                pool.memset(head_avg[q, q], 1.0 / D).then_inc(s_masks, 1)
            pool.wait_ge(s_masks, 9)
            pool.iota(prio_i, pattern=[[-1, N]], base=ZROW, channel_multiplier=0)\
                .then_inc(s_const, 1)
            pool.wait_ge(s_zero, 16 * B)

            def phase(p, kind=None):
                k = p if kind is None else kind
                if not 0 <= k < B:
                    return
                pool.wait_ge(table_stored, 16 * (p + 1))
                for i in range(T):
                    pool.wait_ge(index_ready, p * T + i + 1)
                    if i >= 2 or k > 0:
                        pool.wait_ge(fetched_read, p * T + i - 1)
                    wait(pool, tile_begun, p * T + i)
                    pool.tensor_tensor(ready[:, :], zrow[0:1, 0:1], zrow[0:1, 0:1], ALU.add)\
                        .then_inc(tile_begun, 1)
                    for r in range(TOP):
                        pool.indirect_dma_start(
                            fetched[i % 2][:, r, :], None, table[:, :],
                            bass.IndirectOffsetOnAxis(ap=index[:, i, r:r + 1], axis=0))\
                            .then_inc(gather_in[i % 2], 16)

            phases(pool, phase, None)

        @block.scalar
        def _(act):
            act.dma_start(b_gnn[:, :], gnn_b).then_inc(s_wload2, 16)
            act.dma_start(b_hlrow[:, :], hl_brow).then_inc(s_wload2, 16)
            act.dma_start(w_gate[:, :, :], gate_t).then_inc(s_wload2, 16)
            act.dma_start(w_fg[:, :], fgate_t).then_inc(s_wload2, 16)
            act.dma_start(b_gate[:, :, :], gate_b.partition_broadcast(P)).then_inc(s_wload2, 16)
            for r in range(4):
                q = slice(D * r, D * r + D)
                act.dma_start(b_hlrep[q, :], hl_bcol).then_inc(s_wload2, 16)
                for name, src in (("ln_g", ln_g), ("ln_b", ln_b), ("fc1_b", fc1_b),
                                  ("fc2_b", fc2_b), ("fn_g", fn_g), ("fn_b", fn_b)):
                    act.dma_start(cols[name][q, :], src).then_inc(s_wload2, 16)
            act.wait_ge(s_wload2, 16 * (5 + 4 * 7))
            act.wait_ge(s_const, 3)

            def post(stage):
                if stage == "std":
                    act.wait_ge(post_dve, at(POST_DVE, "aggr"))
                    act.activation(rstd2[:, :], mv2[:, :, 1], ACT.Sqrt, bias=eps[:, 0:1])\
                       .then_inc(post_act, 1)
                    return
                dst = {"agg": agg_t, "xn": xn_t, "xt": xn2_t}[stage]
                for h in range(2):
                    act.wait_ge(post_pe, at(POST_PE, f"{stage}{h}"))
                    act.activation(dst[:, h * HALF:(h + 1) * HALF], MX[h][:, :], ACT.Copy)\
                       .then_inc(post_act, 1)

            def project(n, key):
                act.wait_ge(job_pe, job_at(n, key))
                ps = job_bank(n, key)
                h = 0 if key == "v" else int(key[-1])
                c = slice(h * HALF, (h + 1) * HALF)
                if key[:2] == "sx":
                    if n >= 2:
                        act.wait_ge(out_dve, 2 * (n - 1))
                    for dst in (sx_rep[n % 2], sx_st):
                        act.activation(dst[:, c], ps[:, :], ACT.Identity, bias=b_hlrep[:, n:n + 1])\
                           .then_inc(proj_act, 1)
                elif key == "v":
                    act.activation(v_sb[n % 2][:, :, :], ps[:, 0:T * D]
                                   .rearrange("p (t d) -> p t d", d=D), ACT.Copy).then_inc(proj_act, 1)
                else:
                    dst = k_st[n % 2][0:96, c] if key[0] == "k" else q_st[n % 2][:, int(key[1]), c]
                    act.activation(dst, ps[0:96 if key[0] == "k" else P, :], ACT.Copy)\
                       .then_inc(proj_act, 1)

            def gate(n):
                act.wait_ge(gate_dve, gate_at(n, "sub"))
                act.activation(lg_e[:, :, :], lg_s[:, :, :], ACT.Exp).then_inc(gate_act, 1)

            def max_rows(b, n, k):
                act.wait_ge(job_pe, job_at(n, "m"))
                if not (k == 1 and n == 0):
                    act.wait_ge(mrow_in, 16 * (b * NH + n))
                act.activation(mrow[:, :], job_bank(n, "m")[0:NE * T, 0:P], ACT.Copy, scale=-1.0)\
                   .then_inc(mrow_act, 1)

            def denominators(n, h):
                act.wait_ge(pv_pe, n * NG + LASTG[h] + 1)
                if h == 0 and n > 0:
                    act.wait_ge(job_pe, job_at(n - 1, "lg"))
                act.activation(den_t[:, h * HALF:(h + 1) * HALF], PVD[:, :], ACT.Copy)\
                   .then_inc(den_act, 1)

            def exps(b, n, k):
                for t in range(NT):
                    g, e = divmod(t, NE)
                    for m, key in JOB_AT[n].get(t, []):
                        if m == n + 1:
                            project(m, key)
                        elif key == "row1":
                            gate(m)
                    if e == 0 and n == NH - 1 and k < B and g in POST_ACT_AT:
                        post(POST_ACT_AT[g])
                    if n == NH - 1 and k == B:
                        for stage in TAIL_ACT_AT.get(t, []):
                            tail(TAIL2, stage)
                    if t == NE * (LASTG[0] + 2):
                        denominators(n, 0)
                    w = 512 - STG[g][2]
                    act.wait_ge(st_pe, n * NT + t + 1)
                    if e == 0 and n * NG + g >= 2:
                        act.wait_ge(pv_pe, n * NG + g - 1)
                    act.activation(probs[t % NP][:, 0:w], ST[t % 2][:, 0:w], ACT.Exp, scale=SCALE)\
                       .then_inc(exp_act, 1)
                denominators(n, 1)

            def tail(u, stage):
                dst, src, func, s, names, key, kw = {
                    "t": (u.yt, None, ACT.Copy, u.pe, T_PE, "t", {}),
                    "sq": (u.sq, u.yc, ACT.Square, u.dve, T_DVE, "yc", {}),
                    "l1": (u.rs, None, ACT.Ln, u.pe, T_PE, "v1", {"bias": eps[:, 1:2]}),
                    "s1": (u.rs, u.rs, ACT.Exp, u.act, T_ACT, "l1", {"scale": -0.5}),
                    "fx": (u.fx, u.y, ACT.Identity, u.dve, T_DVE, "yn",
                           {"scale": cols["ln_g"][:, :], "bias": cols["ln_b"][:, :]}),
                    "r1": (u.r, None, ACT.Relu, u.pe, T_PE, "h1", {"bias": cols["fc1_b"][:, :]}),
                    "r2": (u.r, None, ACT.Identity, u.pe, T_PE, "h2", {"bias": cols["fc2_b"][:, :]}),
                    "sz": (u.sq, u.yc, ACT.Square, u.dve, T_DVE, "zc", {}),
                    "l2": (u.rs, None, ACT.Ln, u.pe, T_PE, "v2", {"bias": eps[:, 1:2]}),
                    "s2": (u.rs, u.rs, ACT.Exp, u.act, T_ACT, "l2", {"scale": -0.5}),
                    "fo": (u.fo, u.y, ACT.Identity, u.dve, T_DVE, "zn",
                           {"scale": cols["fn_g"][:, :], "bias": cols["fn_b"][:, :]}),
                    "ex": (None, None, ACT.Exp, u.dve, T_DVE, "ls", {}),
                }[stage]
                for h in range(2):
                    c, ts = slice(h * HALF, (h + 1) * HALF), slice(4 * h, 4 * h + 4)
                    act.wait_ge(s, at(names, f"{key}{h}"))
                    if stage == "ex":
                        act.activation(u.l[:, 1, ts, :], u.l[:, 0, ts, :], func).then_inc(u.act, 1)
                    else:
                        act.activation(dst[:, c], u.bank[h][:, :] if src is None else src[:, c], func, **kw)\
                           .then_inc(u.act, 1)

            def phase(p, kind=None):
                k = p if kind is None else kind
                att = 1 <= k <= B
                if att:
                    for key in PROJ:
                        project(0, key)
                if k < B - 1:
                    act.wait_ge(pre_step, 2)
                    act.activation(rstd[:, :], mv[:, :, 1], ACT.Sqrt, bias=eps[:, 0:1])\
                       .then_inc(pre_act, 1)
                for t in range(NT):
                    if k >= LAG:
                        for stage in TAIL_ACT_AT.get(t, []):
                            for u in (TAIL1, TAIL2) if k > B else (TAIL1,):
                                tail(u, stage)
                    if att:
                        for n, key in JOB_AT[-1].get(t, []):
                            project(n, key)
                if att:
                    b = p - 1
                    max_rows(b, 0, k)
                    for n in range(NH):
                        exps(b, n, k)
                        if n + 1 < NH:
                            max_rows(b, n + 1, k)
                    gate(NH - 1)
                elif k == 0:
                    for stage in POST_ACT_AT.values():
                        post(stage)

            phases(act, phase, BARRIER[1])

        @block.tensor
        def _(pe):
            mm = pe.matmul
            pe.wait_ge(s_wload, 16 * (2 + 12 + 8))
            pe.wait_ge(s_wload2, 16 * (5 + 4 * 7))
            pe.wait_ge(s_const, 3)
            pe.wait_ge(s_wready, 5)

            def job(n, k):
                if BEFORE[n, k]:
                    pe.wait_ge(*job_freed(*BEFORE[n, k]))
                return job_bank(n, k)

            def project(b, n, key):
                ps = job(n, key)
                h = 0 if key == "v" else int(key[-1])
                c = slice(h * HALF, (h + 1) * HALF)
                if key[:2] == "sx":
                    m = mm(ps[:, :], w_hlrep[:, n, :, :].rearrange("p r d -> p (r d)"), xn2_t[:, c],
                           start=True, stop=True)
                elif key == "v":
                    for t in range(T):
                        m = mm(ps[:, t * D:(t + 1) * D], sx_st[:, t * P:(t + 1) * P], w_v[:, n, :],
                               start=True, stop=True)
                else:
                    if key[0] == "k":
                        pe.wait_ge(proj_dve, pdve_at(n, f"sx{h}"))
                    w = w_k[:, n, :, :] if key[0] == "k" else w_q[:, n * NE + int(key[1]), :, :]
                    m = mm(ps[0:96 if key[0] == "k" else P, :], w.rearrange("p r d -> p (r d)"), sx_st[:, c],
                           start=True, stop=True)
                m.then_inc(job_pe, 1)

            def max_tile(b, n, t, k):
                e, m = divmod(t, len(MAXT))
                i, kb, w = MAXT[m]
                g = n * NT + t
                if t == 0:
                    pe.wait_ge(proj_dve, pdve_at(n, f"q{NE - 1}1"))
                if g >= 2:
                    pe.wait_ge(mx_dve, g - 1)
                ps = MX[t % 2]
                diag = P * i // 512 == kb
                last = mm(ps[:, 0:w], q_st[n % 2][:, e, i * P:(i + 1) * P],
                          k_st[n % 2][:, 512 * kb:512 * kb + w], start=True, stop=not diag)
                if diag:
                    last = mm(ps[:, w - P:w], identb[:, :], mask_qk[:, :], start=False, stop=True)
                last.then_inc(mx_pe, 1)

            def score_tile(b, n, t, k):
                g, e = divmod(t, NE)
                h, j, off = STG[g]
                w = 512 - off
                if t == 0:
                    pe.wait_ge(mrow_in, 16 * (b * NH + n + 1))
                u = n * NT + t
                if u >= 2:
                    pe.wait_ge(exp_act, u - 1)
                ps = ST[t % 2]
                diag = j >= 4 * h
                last = mm(ps[:, 0:w], k_st[n % 2][:, j * P:(j + 1) * P],
                          q_st[n % 2][:, e, h * HALF + off:(h + 1) * HALF], start=True, stop=not diag)
                if diag:
                    last = mm(ps[:, 0:P], identb[:, :], mask_kq[:, :], start=False, stop=True)
                last.then_inc(st_pe, 1)

            def values(n, g):
                h, j, off = STG[g]
                pe.wait_ge(exp_act, n * NT + NE * (g + 1))
                if j == 0 and n + h > 0:
                    pe.wait_ge(out_dve, n * 2 + h)
                for e in range(NE):
                    mm(PVO[D * e:D * e + D, off:512], v_sb[n % 2][:, j, :],
                       probs[(NE * g + e) % NP][:, 0:512 - off], start=j == 0, stop=g == LASTG[h])

            def sums(n, g):
                h, j, off = STG[g]
                if j == 0 and n + h > 0:
                    pe.wait_ge(den_act, n * 2 + h)
                for e in range(NE):
                    last = mm(PVD[D * e:D * e + D, off:512], ones_den[:, :],
                              probs[(NE * g + e) % NP][:, 0:512 - off], start=j == 0, stop=g == LASTG[h])
                last.then_inc(pv_pe, 1)

            def max_rows(n):
                pe.wait_ge(comb_dve, n + 1)
                ps = job(n, "m")
                pe.transpose(ps[0:NE * T, 0:P], mx[:, :, :].rearrange("p e t -> p (e t)"), ident[:, :])\
                  .then_inc(job_pe, 1)

            def gate(b, n, key):
                if key == "lg":
                    pe.wait_ge(out_dve, n * 2 + 2)
                    pe.wait_ge(den_act, n * 2 + 2)
                    ps = job(n, key)
                    for t in range(T):
                        q = LG * t
                        mm(ps[:, q:q + NE * NE], o_t[:, t * P:(t + 1) * P],
                           w_gatex[:, n, :, :].rearrange("p g e -> p (g e)"), start=True, stop=True)
                        m = mm(ps[:, q + NE * NE:q + LG], den_t[:, t * P:(t + 1) * P], pick[:, :],
                               start=True, stop=True)
                else:
                    h = int(key[-1])
                    ps = job(n, key)
                    for t in range(4):
                        m = pe.transpose(ps[:, t * P:(t + 1) * P],
                                         o_t[:, h * HALF + t * P:h * HALF + (t + 1) * P], ident[:, :])
                m.then_inc(job_pe, 1)

            def warm(n):
                if n:
                    pe.wait_ge(exp_act, n * NT)
                for _ in range(WARM):
                    mm(ST[0][:, :], identb[:, :], mask_kq[:, :].unsqueeze(1).broadcast_to([P, 4, P]), start=True, stop=True)

            def attention(b, k):
                for key in PROJ:
                    project(b, 0, key)
                for t in range(NT):
                    if k >= LAG and t % TAIL_EVERY == TAIL_EVERY - 1:
                        tail(TAIL1, TAIL_PE[t // TAIL_EVERY])
                    for n, key in JOB_AT[-1].get(t, []):
                        project(b, n, key)
                    max_tile(b, 0, t, k)
                if k >= LAG:
                    pe.wait_ge(tail_dve, at(T_DVE, "om1"))
                max_rows(0)
                for n in range(NH):
                    warm(n)
                    for t in range(NT):
                        for m, key in JOB_AT[n].get(t, []):
                            if m == n + 1:
                                project(b, m, key)
                            else:
                                gate(b, m, key)
                        if n == NH - 1 and k == B and t % TAIL_EVERY == TAIL_EVERY - 1:
                            tail(TAIL2, TAIL_PE[t // TAIL_EVERY])
                        if n == NH - 1 and k < B and t % NE == 0 and t // NE in POST_PE_AT:
                            post(b + 1, k, POST_PE_AT[t // NE])
                        score_tile(b, n, t, k)
                        for m in max_tiles(n, t):
                            max_tile(b, n + 1, m, k)
                        if t >= NE and t % NE == 1:
                            values(n, t // NE - 1)
                        elif t >= NE and t % NE == 3:
                            sums(n, t // NE - 1)
                    values(n, NG - 1)
                    sums(n, NG - 1)
                    if n + 1 < NH:
                        max_rows(n + 1)
                for key in GATE:
                    gate(b, NH - 1, key)

            def post(b, k, stage):
                if stage == "resid" and k >= LAG:
                    return
                if stage == "agg":
                    pe.wait_ge(neigh_dve, T)
                    if k >= 1:
                        pe.wait_ge(comb_dve, NH)
                elif stage == "xn":
                    pe.wait_ge(rows_in, 32 * (b + 1))
                elif stage == "xt":
                    pe.wait_ge(post_dve, at(POST_DVE, "xn2"))
                for h in range(2):
                    if stage in ("xn", "h"):
                        pe.wait_ge(post_act, at(POST_ACT, f"{'agg' if stage == 'xn' else 'xn'}{h}"))
                    if stage == "resid":
                        pe.wait_ge(post_act, at(POST_ACT, f"xt{h}"))
                    for t in range(4):
                        i = 4 * h + t
                        c = slice(i * P, (i + 1) * P)
                        ps = MX[h][:, t * P:(t + 1) * P]
                        if stage == "h":
                            mm(ps, xn_t[:, c], w_gnn[:, 0, :], start=True, stop=False)
                            mm(ps, agg_t[:, c], w_gnn[:, 1, :], start=False, stop=False)
                            m = mm(ps, ones_row[:, :], b_gnn[:, :], start=False, stop=True)
                        elif stage == "resid":
                            mm(ps, xn2_t[:, c], w_hl[:, :], start=True, stop=False)
                            m = mm(ps, ones_row[:, :], b_hlrow[:, :], start=False, stop=True)
                        else:
                            src = {"agg": agg, "xn": xnr, "xt": xn2}[stage]
                            m = pe.transpose(ps, src[:, i, :], ident[:, :])
                    m.then_inc(resid_pe if stage == "resid" else post_pe, 1)

            def tail(u, stage):
                c2 = lambda h: slice(int(h) * HALF, (int(h) + 1) * HALF)
                src, w, s, names, key = {
                    "t": (u.y, None, u.dve, T_DVE, "y"),
                    "m1": (u.yt, head_avg, u.act, T_ACT, "t"),
                    "v1": (u.sq, head_avg, u.act, T_ACT, "sq"),
                    "h1": (u.fx, w_fc1, u.act, T_ACT, "fx"),
                    "h2": (u.z, w_fc2, u.dve, T_DVE, "h1"),
                    "m2": (u.z, head_avg, u.dve, T_DVE, "z"),
                    "v2": (u.sq, head_avg, u.act, T_ACT, "sz"),
                    "lg": (u.fo, w_fg, u.act, T_ACT, "fo"),
                    "rw": (u.fo, None, u.dve, T_DVE, "ls"),
                }[stage]
                for h in "01":
                    pe.wait_ge(s, at(names, key + h))
                    ps = u.bank[int(h)]
                    for t in range(4):
                        col = (4 * int(h) + t) * P
                        if w is None:
                            m = pe.transpose(ps[:, t * P:(t + 1) * P], src[:, col:col + P], ident[:, :])
                        elif stage == "lg":
                            m = mm(ps[:, t * NH:(t + 1) * NH], src[:, col:col + P], w[:, :],
                                   start=True, stop=True)
                        elif t == 0:
                            m = mm(ps[:, :], w[:, :], src[:, c2(h)], start=True, stop=True)
                    m.then_inc(u.pe, 1)

            def phase(p, kind=None):
                k = p if kind is None else kind
                if 1 <= k <= B:
                    attention(p - 1, k)
                elif k == 0:
                    for stage in POST_PE_AT.values():
                        post(p, k, stage)
                elif k > B:
                    for stage in TAIL_PE:
                        for u in (TAIL1, TAIL2):
                            tail(u, stage)

            phases(pe, phase, BARRIER[0])

        @block.vector
        def _(dve):
            dve.wait_ge(s_wload, 16 * (2 + 12 + 8))
            dve.wait_ge(s_const, 3)
            dve.wait_ge(s_wload2, 16 * (5 + 4 * 7))
            dve.tensor_copy(prio[:, :], prio_i)
            for e in range(NE):
                q = slice(D * e, D * e + D)
                dve.tensor_copy(w_gatex[q, :, :, e], w_gate[q, :, :])
            for r in range(4):
                dve.tensor_copy(w_hlrep[:, :, r, :], w_hl[:, :].rearrange("p (n d) -> p n d", d=D))
            for i in range(2):
                dve.memset(k_st[i][96:128, :].bitcast(F32), 0.0).then_inc(s_wready, 1)
                dve.wait_ge(s_wready, i + 1)
                dve.memset(k_st[i][96:97, :].bitcast(F32), 1.0)
            dve.memset(w_q[:, :, 3, :].bitcast(F32), 0.0)
            dve.tensor_copy(w_hi[:, :, :], w_in[:, :, :]).then_inc(s_wready, 1)
            dve.wait_ge(s_wready, 3)
            dve.tensor_tensor(w_lo[:, :, :], w_in[:, :, :], w_hi[:, :, :].bitcast(F32), ALU.subtract)\
               .then_inc(s_wready, 1)
            dve.wait_ge(s_wready, 4)
            for r in range(4):
                q = slice(D * r, D * r + D)
                src = (w_hi if r % 2 == 0 else w_lo)
                for c in range(3):
                    dve.tensor_copy(w_q[q, :, c, :], src[q, 0:16, :].bitcast(F32))
                    dve.tensor_copy(w_k[q, :, c, :], src[q, 16:20, :].bitcast(F32))
                last = dve.tensor_copy(w_v[q, :, :], src[q, 20:24, :].bitcast(F32))
            last.then_inc(s_wready, 1)

            def moments(src, st, m, s, base):
                for t in range(T):
                    last = dve.bn_stats(st[:, t, :], src[:, t, :])
                last.then_inc(s, 1)
                dve.wait_ge(s, base + 1)
                for t in range(T):
                    last = dve.bn_aggr(m[:, t, :], st[:, t, :])
                last.then_inc(s, 1)

            def normalise(src, m, rs, dst, s, base, std_act, std_value):
                dve.wait_ge(std_act, std_value)
                dve.reciprocal(rs[:, :], rs[:, :]).then_inc(s, 1)
                dve.wait_ge(s, base + 3)
                for t in range(T):
                    last = dve.tensor_scalar(dst[:, t, :], src[:, t, :], m[:, t, 0:1], rs[:, t:t + 1],
                                             ALU.subtract, ALU.mult)
                last.then_inc(s, 1)

            def pre(b, k):
                dve.wait_ge(x_in, 16 * (b + 1))
                if k >= 0:
                    dve.wait_ge(table_stored, 16 * b)
                moments(xa, stats, mv, pre_step, 0)
                normalise(xa, mv, rstd, xn, pre_step, 0, pre_act, 1)
                if k >= 0:
                    dve.tensor_scalar(prio[:, :], prio[:, :], float(-N), None, ALU.add)\
                       .then_inc(pre_step, 1)

            def rank(b, i, step):
                if step == 0:
                    dve.wait_ge(adj_in[i % 2], (b * (T // 2) + i // 2 + 1) * 16)
                    if i > 0:
                        dve.wait_ge(rank_step, rank_at(i, 0))
                    elif not (isinstance(b, int) and b == 0):
                        dve.wait_ge(pre_step, NORMED + 1)
                    dve.scalar_tensor_tensor(score[:, :], adj_t[i % 2][:, :], 0.0, prio[:, :],
                                             ALU.not_equal, ALU.mult).then_inc(rank_step, 1)
                    return
                dve.wait_ge(rank_step, rank_at(i, step))
                r, what = divmod(step - 1, 2)
                eight = top[:, i, 8 * r:8 * r + 8] if r < ROUNDS else None
                if step == INDEXED:
                    dve.tensor_scalar(index[:, i, :], top[:, i, :], -1.0, float(ZROW),
                                      ALU.mult, ALU.add).then_inc(index_ready, 1)
                elif step == FLOORED:
                    dve.tensor_scalar(floor[:, i:i + 1], top[:, i, TOP:TOP + 1], 0.0, NEG,
                                      ALU.is_gt, ALU.mult).then_inc(rank_step, 1)
                elif what == 0:
                    dve.max(eight, score[:, :]).then_inc(rank_step, 1)
                else:
                    dve.match_replace(score[:, :], eight, score[:, :], 0.0).then_inc(rank_step, 1)

            def neighbours(b, i, step):
                if step == 0:
                    dve.wait_ge(gather_in[i % 2], (b * (T // 2) + i // 2 + 1) * 16 * TOP)
                    dve.tensor_reduce(agg[:, i, :], fetched[i % 2][:, :, :].rearrange("p r c -> p c r"),
                                      AX.X, ALU.max).then_inc(fetched_read, 1)
                else:
                    dve.wait_ge(fetched_read, b * T + i + 1)
                    dve.tensor_scalar(agg[:, i, :], agg[:, i, :], floor[:, i:i + 1], None, ALU.max)\
                       .then_inc(neigh_dve, 1)

            def gnn_step(p, k, item):
                what, i, r = item
                if what == "max" and 0 <= k < B:
                    neighbours(p, i, r)
                elif what == "rank" and k < B - 1:
                    rank(p + 1, i, r)

            def post(b, k, stage):
                base = at(POST_DVE, "x21")
                if stage == "x2":
                    for h in range(2):
                        dve.wait_ge(post_pe, at(POST_PE, f"h{h}"))
                        if h == 0:
                            dve.wait_ge(rows_in, 32 * (b + 1))
                            if k >= 1:
                                dve.wait_ge(x2_stored, 16 * b)
                        ts = slice(4 * h, 4 * h + 4)
                        dve.scalar_tensor_tensor(x2[:, ts, :],
                                                 MX[h][:, :].rearrange("p (t c) -> p t c", c=C), 0.0,
                                                 xr[:, ts, :], ALU.max, ALU.add).then_inc(post_dve, 1)
                    dve.wait_ge(post_dve, base)
                    moments(x2, stats2, mv2, post_dve, base)
                elif stage == "xn2":
                    normalise(x2, mv2, rstd2, xn2, post_dve, base, post_act, at(POST_ACT, "std"))
                elif k < LAG:
                    for h in range(2):
                        dve.wait_ge(resid_pe, h + 1)
                        ts = slice(4 * h, 4 * h + 4)
                        src = MX[h][:, :].rearrange("p (t c) -> p t c", c=C)
                        if isinstance(b, int):
                            c = slice(b * D, (b + 1) * D)
                        else:
                            c = bass.ds(b * D, D)
                        dve.tensor_copy(resid[:, ts, c], src[:, :, c]).then_inc(resid_dve, 1)

            def project(n, key):
                if key == "v":
                    return
                c = slice(int(key[-1]) * HALF, (int(key[-1]) + 1) * HALF)
                dve.wait_ge(proj_act, pact_at(n, key))
                q, full, dst = {
                    "s": (slice(64, 128), sx_rep[n % 2][:, c], sx_st[:, c]),
                    "k": (slice(32, 64), job_bank(n, key)[:, :], k_st[n % 2][:, c]),
                    "q": (slice(64, 96), job_bank(n, key)[:, :],
                          q_st[n % 2][:, int(key[1]) if key[0] == "q" else 0, c]),
                }[key[0]]
                dve.tensor_tensor(dst[q], full[q], dst[q].bitcast(F32), ALU.subtract)\
                   .then_inc(proj_dve, 1)

            def max_tile(b, n, t):
                e, m = divmod(t, len(MAXT))
                i, kb, w = MAXT[m]
                dve.wait_ge(mx_pe, n * NT + t + 1)
                dst = mx[:, e, i:i + 1] if kb == 0 else mxb[:, e, i - 4:i - 3]
                dve.tensor_reduce(dst, MX[t % 2][:, 0:w], AX.X, ALU.max).then_inc(mx_dve, 1)

            def combine(b, n):
                dve.wait_ge(mx_dve, (n + 1) * NT)
                dve.tensor_tensor(mx[:, :, 4:8], mx[:, :, 4:8], mxb[:, :, :], ALU.max)\
                   .then_inc(comb_dve, 1)

            def outputs(b, n, h):
                c = slice(h * HALF, (h + 1) * HALF)
                dve.wait_ge(pv_pe, n * NG + LASTG[h] + 1)
                dve.scalar_tensor_tensor(o_t[:, c], sx_rep[n % 2][:, c], 0.0, PVO[:, :],
                                         ALU.not_equal, ALU.mult).then_inc(out_dve, 1)

            def over(small, like):
                return small.unsqueeze(len(small.shape)).broadcast_to(like)

            def softmax4(src, work, part, exped, dst, s, a_sem, a_value, at_step, keys):
                t = src.shape[1]
                dve.tensor_reduce(part[0], src, AX.X, ALU.max).then_inc(s, 1)
                dve.wait_ge(s, at_step(keys[0]))
                dve.tensor_tensor(work, src, over(part[0], [P, t, 4]), ALU.subtract).then_inc(s, 1)
                dve.wait_ge(a_sem, a_value)
                dve.tensor_reduce(part[1], exped, AX.X, ALU.add).then_inc(s, 1)
                dve.wait_ge(s, at_step(keys[2]))
                dve.reciprocal(part[2], part[1]).then_inc(s, 1)
                dve.wait_ge(s, at_step(keys[3]))
                dve.tensor_tensor(dst, exped, over(part[2], [P, t, 4]), ALU.mult).then_inc(s, 1)
                dve.wait_ge(s, at_step(keys[4]))

            def gate(b, n, k):
                step = lambda key: gate_at(n, key)
                dve.wait_ge(job_pe, job_at(n, "lg"))
                lgs = job_bank(n, "lg")[:, 0:T * LG].rearrange("p (t c) -> p t c", c=LG)
                dve.reciprocal(rden[:, :, :], lgs[:, :, NE * NE:LG]).then_inc(gate_dve, 1)
                dve.wait_ge(gate_dve, step("rd"))
                dve.tensor_tensor(part_lg[:, :, :, :],
                                  lgs[:, :, 0:NE * NE].rearrange("p t (g e) -> p t g e", e=NE),
                                  rden[:, :, :].unsqueeze(2).broadcast_to([P, T, NE, NE]), ALU.mult)\
                   .then_inc(gate_dve, 1)
                dve.wait_ge(gate_dve, step("pl"))
                dve.tensor_reduce(lg[:, :, :], part_lg[:, :, :, :], AX.X, ALU.add).then_inc(gate_dve, 1)
                dve.wait_ge(gate_dve, step("sl"))
                dve.tensor_tensor(lg[:, :, :], lg[:, :, :],
                                  b_gate[:, n:n + 1, :].broadcast_to([P, T, NE]), ALU.add)\
                   .then_inc(gate_dve, 1)
                dve.wait_ge(gate_dve, step("lg"))
                softmax4(lg[:, :, :], lg_s[:, :, :], [g8[:, j, :] for j in range(3)], lg_e[:, :, :],
                         gs[:, :, :], gate_dve, gate_act, n + 1, step,
                         ["max", "sub", "sum", "rec", "gs"])
                dve.tensor_tensor(gs[:, :, :], gs[:, :, :], rden[:, :, :], ALU.mult).then_inc(gate_dve, 1)
                dve.wait_ge(gate_dve, step("gr"))
                if n == 0 and k != 1:
                    dve.wait_ge(mix_stored, 16 * b)
                for h in range(2):
                    dve.wait_ge(job_pe, job_at(n, f"row{h}"))
                    ts = slice(4 * h, 4 * h + 4)
                    c = slice(h * HALF, (h + 1) * HALF)
                    dve.tensor_tensor(wmix[:, c].rearrange("p (t d) -> p t d", d=D),
                                      job_bank(n, f"row{h}")[:, :].rearrange("p (t d) -> p t d", d=D),
                                      over(gs[:, ts, :].rearrange("p t e -> p (t e)"), [P, 16, D]),
                                      ALU.mult).then_inc(gate_dve, 1)
                    dve.wait_ge(gate_dve, step(f"w{h}"))
                    dve.tensor_reduce(mixed[:, ts, n, :], wmix[:, c]
                                      .rearrange("p (t e d) -> p t d e", e=NE, d=D),
                                      AX.X, ALU.add).then_inc(gate_dve, 1)

            def attention(p, k):
                b = p - 1
                for key in PROJ:
                    project(0, key)
                if k < B - 1:
                    pre(p + 1, k)
                for t in range(NT):
                    if k >= LAG and t % TAIL_EVERY == 0:
                        tail(TAIL1, p - LAG + 1, TAIL_DVE[t // TAIL_EVERY])
                    for n, key in JOB_AT[-1].get(t, []):
                        project(n, key)
                    max_tile(b, 0, t)
                    for item in gnn_steps(-1, t):
                        gnn_step(p, k, item)
                combine(b, 0)
                for n in range(NH):
                    for t in range(NT):
                        for m, key in JOB_AT[n].get(t, []):
                            if m == n + 1:
                                project(m, key)
                            elif key == "row1":
                                gate(b, m, k)
                        if n == NH - 1 and k == B and t % TAIL_EVERY == 0:
                            tail(TAIL2, 1, TAIL_DVE[t // TAIL_EVERY])
                        for m in max_tiles(n, t):
                            max_tile(b, n + 1, m)
                        for item in gnn_steps(n, t):
                            gnn_step(p, k, item)
                        if t == NE * (LASTG[0] + 2):
                            outputs(b, n, 0)
                        if n == NH - 1 and k < B and t % NE == 0 and t // NE in POST_DVE_AT:
                            post(p, k, POST_DVE_AT[t // NE])
                    if n + 1 < NH:
                        combine(b, n + 1)
                    outputs(b, n, 1)
                gate(b, NH - 1, k)

            def tail(u, loads, stage):
                c2 = lambda h: slice(int(h) * HALF, (int(h) + 1) * HALF)
                r3 = lambda t_, h: t_[:, c2(h)].rearrange("p (t c) -> p t c", c=C)
                psl = lambda h: u.bank[h][:, 0:4 * NH].rearrange("p (t n) -> p t n", n=NH)
                r4 = lambda a: a.rearrange("p (g d) -> p g d", d=D)
                hs = [slice(0, 4), slice(4, 8)]

                def did(i):
                    i.then_inc(u.dve, 1)

                def mine(key):
                    dve.wait_ge(u.dve, at(T_DVE, key))

                if stage == "y":
                    dve.wait_ge(u.loaded, 32 * loads)
                    for h in range(2):
                        did(dve.tensor_tensor(r3(u.y, h), u.m[:, hs[h], :], resid[:, hs[h], :], ALU.add))
                elif stage in ("yc", "zc"):
                    for h in "01":
                        dve.wait_ge(u.pe, at(T_PE, ("m1" if stage == "yc" else "m2") + h))
                        did(dve.tensor_tensor(u.yc[:, c2(h)], (u.yt if stage == "yc" else u.z)[:, c2(h)],
                                              u.bank[int(h)][:, :], ALU.subtract))
                elif stage in ("yn", "zn"):
                    for h in "01":
                        dve.wait_ge(u.act, at(T_ACT, ("s1" if stage == "yn" else "s2") + h))
                        did(dve.tensor_tensor(u.y[:, c2(h)], u.yc[:, c2(h)], u.rs[:, c2(h)], ALU.mult))
                elif stage in ("h1", "h2"):
                    for h in "01":
                        dve.wait_ge(u.act, at(T_ACT, ("r1" if stage == "h1" else "r2") + h))
                        did(dve.scalar_tensor_tensor(u.z[:, c2(h)], u.fx[:, c2(h)], 0.0, u.r[:, c2(h)],
                                                     ALU.not_equal, ALU.mult))
                    if stage == "h2":
                        for h in "01":
                            mine("h2" + h)
                            did(dve.tensor_tensor(u.z[:, c2(h)], u.z[:, c2(h)], u.fx[:, c2(h)], ALU.add))
                elif stage == "soft":
                    for h in range(2):
                        dve.wait_ge(u.pe, at(T_PE, f"lg{h}"))
                        did(dve.tensor_reduce(u.s8[:, 0, hs[h]], psl(h), AX.X, ALU.max))
                    for h in range(2):
                        mine(f"lm{h}")
                        did(dve.tensor_tensor(u.l[:, 0, hs[h], :], psl(h),
                                              over(u.s8[:, 0, hs[h]], [P, 4, NH]), ALU.subtract))
                elif stage == "out":
                    for h in range(2):
                        dve.wait_ge(u.act, at(T_ACT, f"ex{h}"))
                        did(dve.tensor_reduce(u.s8[:, 1, hs[h]], u.l[:, 1, hs[h], :], AX.X, ALU.add))
                    for h in range(2):
                        mine(f"su{h}")
                        did(dve.reciprocal(u.s8[:, 2, hs[h]], u.s8[:, 1, hs[h]]))
                    for h in range(2):
                        mine(f"re{h}")
                        did(dve.tensor_tensor(u.l[:, 2, hs[h], :], u.l[:, 1, hs[h], :],
                                              over(u.s8[:, 2, hs[h]], [P, 4, NH]), ALU.mult))
                    for h in range(2):
                        dve.wait_ge(u.pe, at(T_PE, f"rw{h}"))
                        mine(f"gs{h}")
                        did(dve.tensor_tensor(r4(u.y[:, c2(h)]), r4(u.bank[h][:, :]),
                                              over(u.l[:, 2, hs[h], :].rearrange("p t n -> p (t n)"),
                                                   [P, 16, D]), ALU.mult))
                    for h in range(2):
                        mine(f"om{h}")
                        did(dve.tensor_tensor(u.m[:, hs[h], :], r3(u.y, h), u.x[:, hs[h], :], ALU.add))

            def phase(p, kind=None):
                k = p if kind is None else kind
                if 1 <= k <= B:
                    attention(p, k)
                    return
                if k < 1:
                    pre(p + 1, k)
                    for w in GNN:
                        for item in GNN[w]:
                            gnn_step(p, k, item)
                if k == 0:
                    for stage in POST_DVE_AT.values():
                        post(p, k, stage)
                if k > B:
                    for stage in TAIL_DVE:
                        tail(TAIL1, B - LAG + 2, stage)
                        tail(TAIL2, 2, stage)

            phases(dve, phase, BARRIER)


def kernel(x, adj, L0_gnn_W, L0_gnn_b, L0_ffn_hl_w, L0_ffn_hl_b, L0_ffn_wq, L0_ffn_wk, L0_ffn_wv,
           L0_ffn_gate_w, L0_ffn_gate_b, L0_ffn_ln_g, L0_ffn_ln_b, L0_ffn_fc1_w, L0_ffn_fc1_b,
           L0_ffn_fc2_w, L0_ffn_fc2_b, L0_ffn_fnorm_g, L0_ffn_fnorm_b, L0_ffn_fgate_w):
    import numpy as np
    import concourse.bacc as bacc
    from concourse.bass_utils import run_bass_kernel_spmd

    a = lambda v, *shape: np.ascontiguousarray(np.asarray(v).reshape(shape))
    t = lambda v, *axes: np.ascontiguousarray(np.asarray(v).transpose(axes))
    nh, d, h = np.asarray(L0_ffn_hl_w).shape
    ne = np.asarray(L0_ffn_wq).shape[1]
    ins = {
        "x": np.asarray(x), "adj": np.asarray(adj), "gnn_w": np.asarray(L0_gnn_W),
        "gnn_b": a(L0_gnn_b, 1, h),
        "hl_t": t(L0_ffn_hl_w, 2, 0, 1).reshape(h, nh * d),
        "hl_brow": a(L0_ffn_hl_b, 1, nh * d), "hl_bcol": t(L0_ffn_hl_b, 1, 0),
        "wq_t": t(L0_ffn_wq, 3, 0, 1, 2).reshape(d, nh * ne, d),
        "wk_t": t(L0_ffn_wk, 2, 0, 1), "wv_t": t(L0_ffn_wv, 2, 0, 1),
        "gate_t": t(L0_ffn_gate_w, 2, 0, 1), "gate_b": np.asarray(L0_ffn_gate_b),
        "ln_g": a(L0_ffn_ln_g, d, 1), "ln_b": a(L0_ffn_ln_b, d, 1),
        "fc1_t": t(L0_ffn_fc1_w, 1, 0), "fc1_b": a(L0_ffn_fc1_b, d, 1),
        "fc2_t": t(L0_ffn_fc2_w, 1, 0), "fc2_b": a(L0_ffn_fc2_b, d, 1),
        "fn_g": a(L0_ffn_fnorm_g, d, 1), "fn_b": a(L0_ffn_fnorm_b, d, 1),
        "fgate_t": t(L0_ffn_fgate_w, 1, 0),
    }
    nc = bacc.Bacc("TRN2", target_bir_lowering=False, num_devices=1)
    args = [nc.dram_tensor(f"in_{k}", v.shape, mybir.dt.from_np(v.dtype), kind="ExternalInput").ap()
            for k, v in ins.items()]
    out = nc.dram_tensor("out", ins["x"].shape, mybir.dt.float32, kind="ExternalOutput").ap()
    build(nc, *args, out)
    r = run_bass_kernel_spmd(nc, [{f"in_{k}": v for k, v in ins.items()}], core_ids=[0])
    return r.results[0]["out"]
```
